# Optimizing a Trainium2 kernel written in Bass

```python
import numpy as np
import jax
import jax.numpy as jnp

def _softmax(x, axis=-1):
    return jax.nn.softmax(x, axis=axis)

def _gelu(x):
    return jax.nn.gelu(x, approximate=True)

def _silu(x):
    return jax.nn.silu(x)

def _sigmoid(x):
    return jax.nn.sigmoid(x)

def _layernorm(x, axis=-1, eps=1e-05):
    m = jnp.mean(x, axis=axis, keepdims=True)
    v = jnp.var(x, axis=axis, keepdims=True)
    return (x - m) / jnp.sqrt(v + eps)

def _scatter_add(tgt, idx, src, axis=0):
    return tgt.at[idx].add(src)

def _segment_sum(src, seg, n):
    return jax.ops.segment_sum(src, seg, n)
kernel_name = 'mk_adj_ffn_d1_adj_r2_925aa3'

def setup_inputs(seed: int=0):
    np.random.seed(seed)
    _w = jnp.asarray

    def _rec_inputs():
        import jax
        import jax.numpy as jnp
        _gk = jax.random.key(seed)
        x = -0.0003929 + 0.9999 * jax.random.normal(jax.random.fold_in(_gk, 1), (64, 128, 256), jnp.float32)
        _a = jax.random.bernoulli(jax.random.fold_in(_gk, 2), 0.0625, (128, 128))
        _a = jnp.logical_or(_a, jnp.swapaxes(_a, -1, -2))
        _a = jnp.logical_or(_a, jnp.eye(128, dtype=bool))
        _af = _a.astype(jnp.float32)
        _af = _af * jax.random.uniform(jax.random.fold_in(_gk, 3), (128, 128), jnp.float32, 0.05, 1)
        adj = _af
        return (x, adj)
    x, adj = _rec_inputs()

    def _L0_gnn_setup():
        import jax, jax.numpy as jnp
        import numpy as np
        B, N, F_IN, F_OUT = (16, 1024, 256, 256)
        key = jax.random.key(seed)
        k1, k2, k3 = jax.random.split(key, 3)
        x = jax.random.normal(k1, (B, N, F_IN), dtype=jnp.float32)
        adj = jax.random.uniform(k2, (N, N), dtype=jnp.float32)
        bound = np.sqrt(6.0 / F_OUT)
        weight = jax.random.uniform(k3, (F_IN, F_OUT), dtype=jnp.float32, minval=-bound, maxval=bound)
        bias = jnp.zeros((F_OUT,), dtype=jnp.float32)
        return {'x': x, 'adj': adj, 'weight': weight, 'bias': bias}
    _L0_gnn_all = _L0_gnn_setup()
    _L0_gnn_in = {k: v for k, v in _L0_gnn_all.items() if k in ('weight', 'bias')}
    del _L0_gnn_all

    def _L0_ffn_setup():
        import jax, jax.numpy as jnp
        import numpy as np
        D_MODEL = 256
        NUM_EXPERTS = 8
        TOP_K = 2
        FFN_MULT = 2
        HIDDEN = FFN_MULT * D_MODEL
        BATCH, SEQ = (4, 1024)
        key = jax.random.key(seed)
        k_x, k_g, k_bg, k_w1, k_w3, k_w2 = jax.random.split(key, 6)
        sd = 1.0 / np.sqrt(D_MODEL).astype(np.float32)
        sh = 1.0 / np.sqrt(HIDDEN).astype(np.float32)
        return {'x': jax.random.normal(k_x, (BATCH, SEQ, D_MODEL), dtype=jnp.float32), 'Wg': jax.random.normal(k_g, (D_MODEL, NUM_EXPERTS), dtype=jnp.float32) * sd, 'bg': jax.random.normal(k_bg, (NUM_EXPERTS,), dtype=jnp.float32) * 0.01, 'W1': jax.random.normal(k_w1, (NUM_EXPERTS, D_MODEL, HIDDEN), dtype=jnp.float32) * sd, 'W3': jax.random.normal(k_w3, (NUM_EXPERTS, D_MODEL, HIDDEN), dtype=jnp.float32) * sd, 'W2': jax.random.normal(k_w2, (NUM_EXPERTS, HIDDEN, D_MODEL), dtype=jnp.float32) * sh}
    _L0_ffn_all = _L0_ffn_setup()
    _L0_ffn_in = {k: v for k, v in _L0_ffn_all.items() if k in ('Wg', 'bg', 'W1', 'W3', 'W2')}
    del _L0_ffn_all
    return {'x': x, 'adj': adj, 'L0_gnn_weight': _L0_gnn_in['weight'], 'L0_gnn_bias': _L0_gnn_in['bias'], 'L0_ffn_Wg': _L0_ffn_in['Wg'], 'L0_ffn_bg': _L0_ffn_in['bg'], 'L0_ffn_W1': _L0_ffn_in['W1'], 'L0_ffn_W3': _L0_ffn_in['W3'], 'L0_ffn_W2': _L0_ffn_in['W2']}

def reference(x, adj, L0_gnn_weight, L0_gnn_bias, L0_ffn_Wg, L0_ffn_bg, L0_ffn_W1, L0_ffn_W3, L0_ffn_W2):
    import jax
    import jax.numpy as jnp

    def _L0_gnn_ref(x, adj, weight, bias):
        import jax, jax.numpy as jnp
        import numpy as np
        B, N, F_IN, F_OUT = (16, 1024, 256, 256)
        deg = adj.sum(axis=1)
        deg_inv_sqrt = jnp.where(deg > 0, jax.lax.rsqrt(deg), 0.0)
        norm_adj = adj * deg_inv_sqrt[:, None] * deg_inv_sqrt[None, :]
        support = jnp.einsum('bni,io->bno', x, weight)
        output = jnp.einsum('nm,bmo->bno', norm_adj, support)
        return output + bias

    def _L0_ffn_ref(x, Wg, bg, W1, W3, W2):
        import jax, jax.numpy as jnp
        import numpy as np
        D_MODEL = 256
        NUM_EXPERTS = 8
        TOP_K = 2
        FFN_MULT = 2
        HIDDEN = FFN_MULT * D_MODEL
        BATCH, SEQ = (4, 1024)
        B, S, D = x.shape
        E = Wg.shape[1]
        xt = x.reshape(-1, D)
        T = xt.shape[0]
        logits = xt @ Wg + bg
        top_vals, top_idx = jax.lax.top_k(logits, TOP_K)
        top_probs = jax.nn.softmax(top_vals, axis=-1)
        gate_w = jnp.zeros((T, E), dtype=xt.dtype).at[jnp.arange(T)[:, None], top_idx].add(top_probs)

        def body(y, expert):
            w1, w3, w2, g = expert
            h = jax.nn.silu(xt @ w1) * (xt @ w3)
            return (y + g[:, None] * (h @ w2), None)
        y0 = jnp.zeros_like(xt)
        y, _ = jax.lax.scan(body, y0, (W1, W3, W2, gate_w.T))
        return y.reshape(B, S, D)
    x = x + _L0_gnn_ref(_layernorm(x, axis=-1), adj, L0_gnn_weight, L0_gnn_bias)
    x = x + _L0_ffn_ref(_layernorm(x, axis=-1), L0_ffn_Wg, L0_ffn_bg, L0_ffn_W1, L0_ffn_W3, L0_ffn_W2)
    return x

_drawn_inputs = setup_inputs


def setup_inputs(seed=0):
    import zlib

    import numpy as np

    out = dict(_drawn_inputs(seed))
    spreads = {'L0_gnn_bias': (0.0, 0.1)}
    factors = {}
    for name, (base, spread) in spreads.items():
        noise = np.random.default_rng([zlib.crc32(name.encode()), seed]).standard_normal(out[name].shape)
        drawn = base * np.exp(spread * noise) if base else spread * noise
        out[name] = jnp.asarray(drawn.astype(out[name].dtype))
    for name, factor in factors.items():
        out[name] = (out[name] * factor).astype(out[name].dtype)
    return out
```

```python
from contextlib import ExitStack

import concourse.bass as bass
from concourse import mybir

ALU = mybir.AluOpType
ACT = mybir.ActivationFunctionType
F32 = mybir.dt.float32
F16 = mybir.dt.float16
BF16 = mybir.dt.bfloat16
I32 = mybir.dt.int32
U32 = mybir.dt.uint32
AX_X = mybir.AxisListType.X
MAX_OVER_PARTITIONS = bass.bass_isa.ReduceOp.max

P = 128
EPS = 1e-5


class Steps:

    def __init__(self, engine, semaphore):
        self.engine, self.semaphore, self.at, self.done = engine, semaphore, 0, 0

    def mark(self, instruction):
        instruction.then_inc(self.semaphore, 1)
        self.done += 1

    def wait(self):
        self.engine.wait_ge(self.semaphore, self.at + self.done)

    def link(self, instruction):
        self.mark(instruction)
        self.wait()

    def restart(self, at):
        self.at, self.done = at, 0


def build(nc, x, adj, gnn_w, gnn_b, wg, bg, w1, w3, w2, out):
    B, N, D = x.shape
    E, _, HID = w1.shape
    T = B * N
    TOP = 2
    assert N == P and D == 2 * P and HID == 4 * P and T % (4 * P) == 0
    KC = D // P
    HC = HID // P
    G = 4
    NG = T // (G * P)
    TILE = 2 * P
    NT = T * TOP // TILE + E - 1
    NTP = NT + 1
    REGION = T + TILE
    ROW = D + 8
    TOKEN, MARGIN, FIRST = D, D + 1, D + 2
    PIECE = KC * HID
    SLOT = 3 * PIECE
    assert HC * D == PIECE and NG == 2 * E and NT % 2 == 1
    X_SCALE = 2.0 ** 11
    DVE_LINKS = 38
    DOWN = (5, 7)

    tokens_in = x.rearrange("b n d -> (b n) d")
    routed = nc.dram_tensor("routed", (E * REGION + TILE, ROW), F32).ap()

    with ExitStack() as ctx:
        def sb(name, shape, dt):
            return ctx.enter_context(nc.sbuf_tensor(name, shape, dt))

        def sem(name):
            return ctx.enter_context(nc.semaphore(name))

        bank = [ctx.enter_context(nc.psum_tensor(f"bank{i}", [P, 512], F32)) for i in range(8)]

        ident32 = sb("ident32", [P, P], F32)
        ident16 = sb("ident16", [P, P], F16)
        before = sb("before", [P, P], BF16)
        ones = sb("ones", [P, P], BF16)
        up_to = sb("up_to", [P, E, E], F32)
        descending = sb("descending", [P, E], F32)
        region_of = sb("region_of", [P, E], F32)
        tile_no = sb("tile_no", [P, NTP], F32)
        adj_sb = sb("adj_sb", [P, P], F32)
        adj_t = sb("adj_t", [P, P], F32)
        degree = sb("degree", [P, 4], F32)
        gw_sb = sb("gw_sb", [P, KC, D], F32)
        bias_row = sb("bias_row", [1, 3, D], F32)
        bias_cut = sb("bias_cut", [1, 3, D], BF16)
        bias3 = sb("bias3", [3, D], BF16)
        wg_sb = sb("wg_sb", [P, KC, E], F32)
        wg_scaled = sb("wg_scaled", [P, KC, E], F32)
        bg_sb = sb("bg_sb", [P, E], F32)
        weights = sb("weights", [P, (E + 1) * SLOT], F32)
        halves = weights[:, :].bitcast(F16)
        w_max = sb("w_max", [P, E, 3], F32)
        w_top = sb("w_top", [P, 3], F32)
        w_top_all = sb("w_top_all", [P, 3], F32)
        w_low2 = sb("w_low2", [P, 3], F32)
        w_inv2 = sb("w_inv2", [P, 3], F32)
        w_scale = sb("w_scale", [P, 3], F32)
        silu_scale = sb("silu_scale", [P, 1], F32)
        up_scale = sb("up_scale", [P, 1], F32)
        y_scale = sb("y_scale", [P, 1], F32)
        xg = sb("xg", [P, 2, G, D], F32)
        xn = sb("xn", [P, 2, G, D], F32)
        zt = sb("zt", [P, 2, D], F32)
        h1 = sb("h1", [P, 2, G, D], F32)
        xn2 = sb("xn2", [P, 2, G, D], F32)
        xn2t = sb("xn2t", [P, 2, D], F32)
        rows = sb("rows", [P, 2, G, ROW], F32)
        rows16 = rows[:, :, :, :].bitcast(F16)
        stats = sb("stats", [P, 2, G, 6], F32)
        mean_var = sb("mean_var", [P, 2, G, 2], F32)
        std = sb("std", [P, 2, G], F32)
        inv_std = sb("inv_std", [P, 2, G], F32)
        shift = sb("shift", [P, 2, G], F32)
        logits = sb("logits", [P, G, E], F32)
        rest = sb("rest", [P, G, E], F32)
        is_top = sb("is_top", [P, G, E], F32)
        rank = sb("rank", [P, G, E], F32)
        best = sb("best", [P, TOP, G], F32)
        chosen = sb("chosen", [P, TOP, G], F32)
        onehot = sb("onehot", [P, TOP, G, E], F32)
        picks = sb("picks", [P, G, E], BF16)
        picks_sum = sb("picks_sum", [P, E], F32)
        running = sb("running", [P, 2, E], BF16)
        token = sb("token", [P, G], I32)
        place = sb("place", [P, G, E], F32)
        place_of = sb("place_of", [P, TOP, G, E], F32)
        slot_of = sb("slot_of", [P, TOP, G], F32)
        slot_index = sb("slot_index", [P, 2, TOP, G], U32)
        pad_rows = sb("pad_rows", [P, 2, ROW], F32)
        count = sb("count", [P, E], F32)
        tiles_i = sb("tiles_i", [P, 2, E], I32)
        tiles = sb("tiles", [P, E], F32)
        upto = sb("upto", [P, E, E], F32)
        tiles_end = sb("tiles_end", [P, E], F32)
        past = sb("past", [P, NTP, E], F32)
        past_tiles = sb("past_tiles", [P, NTP, E], F32)
        tile_expert = sb("tile_expert", [P, NTP], F32)
        tile_start = sb("tile_start", [P, NTP], F32)
        tile_tmp = sb("tile_tmp", [P, 4, NTP], F32)
        tile_row = sb("tile_row", [P, NTP], I32)
        tile_weights = sb("tile_weights", [P, NTP], I32)
        pad_at = sb("pad_at", [P, E], I32)
        xr = sb("xr", [P, 2, 2, ROW], F32)
        xr16 = xr[:, :, :, :].bitcast(F16)
        xt = sb("xt", [P, 2, 2, KC, TILE], F16)
        silu = sb("silu", [P, 2, TILE], F32)
        hid = sb("hid", [P, HC, TILE], F32)
        hh = sb("hh", [P, 2, 2, HC, TILE], F16)
        y = sb("y", [P, 2, 2, D], F32)
        target = sb("target", [P, 2, 2], U32)
        own = sb("own", [P, 2, 2], F32)
        margin = sb("margin", [P, 2, 2], F32)
        tanh = sb("tanh", [P, 2, 2], F32)
        gate = sb("gate", [P, 2, 2], F32)

        adj_loaded = sem("adj_loaded")
        gnn_loaded = sem("gnn_loaded")
        router_loaded = sem("router_loaded")
        bias_moved = sem("bias_moved")
        x_loaded = [sem(f"x_loaded{i}") for i in range(2)]
        w_loaded = [sem(f"w_loaded{i}") for i in range(2)]
        h1_stored = [sem(f"h1_stored{i}") for i in range(2)]
        dump_stored = sem("dump_stored")
        blank_stored = sem("blank_stored")
        pads_stored = sem("pads_stored")
        scattered = [sem(f"scattered{i}") for i in range(2)]
        rows_loaded = [sem(f"rows_loaded{i}") for i in range(2)]
        y_added = sem("y_added")
        pool_passed = sem("pool_passed")
        dve_passed = sem("dve_passed")
        pool_step = sem("pool_step")
        dve_step = sem("dve_step")
        consts_ready = sem("consts_ready")
        degree_sum = sem("degree_sum")
        degree_root = sem("degree_root")
        adj_half = sem("adj_half")
        adj_turned = sem("adj_turned")
        bias_cut_ready = sem("bias_cut_ready")
        setup_ready = sem("setup_ready")
        stats1_ready = sem("stats1_ready")
        std1_ready = sem("std1_ready")
        norm1_ready = sem("norm1_ready")
        xn_ready = sem("xn_ready")
        z_ready = sem("z_ready")
        zt_ready = sem("zt_ready")
        gnn_ready = sem("gnn_ready")
        h1_done = sem("h1_done")
        stats2_ready = sem("stats2_ready")
        std2_ready = sem("std2_ready")
        norm2_ready = sem("norm2_ready")
        xn2_ready = sem("xn2_ready")
        high_ready = sem("high_ready")
        low_ready = sem("low_ready")
        turned2 = sem("turned2")
        xn2t_ready = sem("xn2t_ready")
        logits_ready = sem("logits_ready")
        logits_taken = sem("logits_taken")
        picks_ready = sem("picks_ready")
        before_ready = sem("before_ready")
        places_ready = sem("places_ready")
        max_ready = sem("max_ready")
        max_all = sem("max_all")
        scales_ready = sem("scales_ready")
        w_high = sem("w_high")
        w_low = sem("w_low")
        counts_ready = sem("counts_ready")
        pad_at_ready = sem("pad_at_ready")
        tiles_ready = sem("tiles_ready")
        x_turned = sem("x_turned")
        xt_ready = sem("xt_ready")
        own_ready = sem("own_ready")
        gate_ready = sem("gate_ready")
        max_step = sem("max_step")
        scale_step = sem("scale_step")
        table_step = sem("table_step")
        margin_ready = sem("margin_ready")
        tanh_ready = sem("tanh_ready")
        up_ready = sem("up_ready")
        silu_ready = sem("silu_ready")
        hid_ready = sem("hid_ready")
        hid_high = sem("hid_high")
        hid_low = sem("hid_low")
        down_ready = sem("down_ready")
        y_ready = sem("y_ready")

        def phase1_steps(engine, step, between, steps=None, links=0):
            def at(n, par):
                if steps is not None and not isinstance(n, int):
                    steps.restart(base + (n - 1) * links)
                start = steps.done if steps is not None else 0
                step(n, par)
                if steps is not None and not isinstance(n, int):
                    assert steps.done - start == links, (steps.done - start, links)

            step(0, 0)
            base = steps.done if steps is not None else 0
            step(1, 1)
            with engine.Fori(1, NG // 4) as i:
                at(i * 2, 0)
                at(i * 2 + 1, 1)
            between()
            with engine.Fori(NG // 4, NG // 2 - 1) as i:
                at(i * 2, 0)
                at(i * 2 + 1, 1)
            if steps is not None:
                steps.restart(base + (NG - 3) * links)
            step(NG - 2, 0)
            step(NG - 1, 1)
            step(NG, 0)

        def phase2_steps(engine, step):
            step(0, 0)
            step(1, 1)
            with engine.Fori(1, (NT - 1) // 2) as i:
                step(i * 2, 0)
                step(i * 2 + 1, 1)
            step(NT - 1, 0)

        def is_first(n, k=1):
            return isinstance(n, int) and n < k

        block = ctx.enter_context(nc.Block())

        @block.sync
        def _(sp):
            sp.dma_start(adj_sb[:, :], adj).then_inc(adj_loaded, 16)
            sp.dma_start(xg[:, 0, :, :], tokens_in[0:G * P, :].rearrange("(t p) d -> p t d", p=P)
                         ).then_inc(x_loaded[0], 16)
            sp.dma_start(gw_sb[:, :, :], gnn_w.rearrange("(c p) d -> p c d", p=P)).then_inc(gnn_loaded, 16)
            sp.dma_start(bias_row[:, 0, :], gnn_b.rearrange("(a d) -> a d", a=1)).then_inc(gnn_loaded, 16)
            sp.dma_start(wg_sb[:, :, :], wg.rearrange("(c p) e -> p c e", p=P)).then_inc(router_loaded, 16)
            sp.dma_start(bg_sb[:, :], bg.partition_broadcast(P)).then_inc(router_loaded, 16)
            sp.dma_start(xg[:, 1, :, :], tokens_in[G * P:2 * G * P, :].rearrange("(t p) d -> p t d", p=P)
                         ).then_inc(x_loaded[1], 16)
            sp.wait_ge(bias_cut_ready, 1)
            for j in range(3):
                sp.dma_start(bias3[j:j + 1, :], bias_cut[:, j, :]).then_inc(bias_moved, 16)

            def load_weights(e, par, at):
                for j, (w, c) in enumerate(((w1, KC), (w3, KC), (w2, HC))):
                    sp.dma_start(weights[:, bass.ds(at * SLOT + j * PIECE, PIECE)].rearrange("p (c h) -> p c h", c=c),
                                 w[bass.ds(e, 1), :, :].rearrange("e (c p) h -> p (e c) h", p=P)
                                 ).then_inc(w_loaded[par], 16)

            def step(n, par, weights_too=False):
                if weights_too:
                    load_weights(n, par, n + 1)
                sp.wait_ge(h1_done, (n + 1) * G)
                sp.dma_start(out[bass.ds(n * (G * P), G * P), :].rearrange("(t p) d -> p t d", p=P),
                             h1[:, par, :, :]).then_inc(h1_stored[par], 16)
                if isinstance(n, int) and n + 2 >= NG:
                    return
                sp.dma_start(xg[:, par, :, :],
                             tokens_in[bass.ds((n + 2) * (G * P), G * P), :].rearrange("(t p) d -> p t d", p=P)
                             ).then_inc(x_loaded[par], 16)

            step(0, 0, True)
            step(1, 1, True)
            with sp.Fori(1, NG // 4) as i:
                step(i * 2, 0, True)
                step(i * 2 + 1, 1, True)
            with sp.Fori(NG // 4, NG // 2 - 1) as i:
                step(i * 2, 0)
                step(i * 2 + 1, 1)
            step(NG - 2, 0)
            step(NG - 1, 1)

            sp.wait_ge(pad_at_ready, 1)
            for e in range(E):
                at = sp.value_load(pad_at[0:1, e:e + 1], min_val=0, max_val=E * REGION - TILE)
                sp.dma_start(routed[bass.ds(at, TILE), :].rearrange("(c p) w -> p c w", p=P),
                             pad_rows[:, :, :]).then_inc(pads_stored, 16)
            sp.wait_ge(pads_stored, 16 * E)
            sp.wait_ge(blank_stored, 16)
            for par in range(2):
                sp.wait_ge(scattered[par], 16 * TOP * G * NG // 2)
            sp.wait_ge(tiles_ready, 1)

            def load_tile(i, par):
                if not is_first(i, 2):
                    sp.wait_ge(x_turned, i - 1)
                    sp.wait_ge(margin_ready, i - 1)
                at = sp.value_load(tile_row[0:1, bass.ds(i, 1)], min_val=0, max_val=E * REGION)
                sp.dma_start(xr[:, par, :, :],
                             routed[bass.ds(at, TILE), :].rearrange("(c p) w -> p c w", p=P)
                             ).then_inc(rows_loaded[par], 16)

            phase2_steps(sp, load_tile)

        @block.gpsimd
        def _(pool):
            steps = Steps(pool, pool_step)
            nc.gpsimd.memset(ident32[:, :], 0.0)
            nc.gpsimd.memset(ident16[:, :], 0.0)
            nc.gpsimd.memset(before[:, :], 1.0)
            nc.gpsimd.memset(ones[:, :], 1.0)
            nc.gpsimd.memset(up_to[:, :, :], 1.0)
            nc.gpsimd.memset(running[:, 0, :], 0.0)
            nc.gpsimd.memset(rows[:, :, :, D:ROW], 0.0)
            steps.link(nc.gpsimd.memset(pad_rows[:, :, :], 0.0))
            for ident in (ident32, ident16):
                nc.gpsimd.affine_select(out=ident[:, :], in_=ident[:, :], compare_op=ALU.not_equal, fill=1.0,
                                        base=0, pattern=[[-1, P]], channel_multiplier=1)
            nc.gpsimd.affine_select(out=before[:, :], in_=before[:, :], compare_op=ALU.is_gt, fill=0.0,
                                    base=0, pattern=[[1, P]], channel_multiplier=-1)
            nc.gpsimd.affine_select(out=up_to[:, :, :], in_=up_to[:, :, :], compare_op=ALU.is_ge, fill=0.0,
                                    base=0, pattern=[[1, E], [-1, E]], channel_multiplier=0)
            nc.gpsimd.iota(descending[:, :], pattern=[[-1, E]], base=E, channel_multiplier=0,
                           allow_small_or_imprecise_dtypes=True)
            nc.gpsimd.iota(region_of[:, :], pattern=[[REGION, E]], base=0, channel_multiplier=0,
                           allow_small_or_imprecise_dtypes=True)
            nc.gpsimd.iota(tile_no[:, :], pattern=[[1, NTP]], base=0, channel_multiplier=0,
                           allow_small_or_imprecise_dtypes=True)
            nc.gpsimd.iota(token[:, :], pattern=[[P, G]], base=0, channel_multiplier=1)
            nc.gpsimd.iota(pad_rows[:, :, TOKEN].bitcast(I32), pattern=[[P, 2]], base=T,
                           channel_multiplier=1).then_inc(consts_ready, 1)
            pool.wait_ge(consts_ready, 1)
            pool.dma_start(routed[E * REGION:E * REGION + TILE, :].rearrange("(c p) w -> p c w", p=P),
                           pad_rows[:, :, :]).then_inc(blank_stored, 16)
            pool.dma_start(out[T:T + TILE, :].rearrange("(c p) d -> p c d", p=P),
                           pad_rows[:, :, 0:D]).then_inc(dump_stored, 16)

            def scatter(n, par):
                if is_first(n):
                    return
                pool.wait_ge(low_ready, n * G)
                pool.wait_ge(high_ready, n * G)
                pool.wait_ge(places_ready, n)
                pool.sem_inc(pool_passed)
                for t in range(G):
                    for k in range(TOP):
                        pool.indirect_dma_start(
                            routed, bass.IndirectOffsetOnAxis(ap=slot_index[:, 1 - par, k, t:t + 1], axis=0),
                            rows[:, 1 - par, t, :], None).then_inc(scattered[1 - par], 16)

            def maxima():
                pool.wait_ge(max_ready, 1)
                nc.gpsimd.partition_all_reduce(w_top_all[:, :], w_top[:, :], P, MAX_OVER_PARTITIONS
                                               ).then_inc(max_all, 1)

            phase1_steps(pool, scatter, maxima)

            pool.wait_ge(dump_stored, 16)
            for par in range(2):
                pool.wait_ge(h1_stored[par], 16 * NG // 2)

            def add(i, par):
                pool.wait_ge(y_ready, i + 1)
                if not is_first(i):
                    pool.wait_ge(y_added, i * 32)
                pool.sem_inc(pool_passed)
                for c in range(2):
                    pool.indirect_dma_start(
                        out, bass.IndirectOffsetOnAxis(ap=target[:, par, c:c + 1], axis=0),
                        y[:, par, c, :], None, compute_op=ALU.add).then_inc(y_added, 16)

            phase2_steps(pool, add)
            pool.wait_ge(y_added, NT * 32)

        @block.scalar
        def _(act):
            act.wait_ge(degree_sum, 1)
            nc.scalar.activation(degree[:, 2:3], degree[:, 1:2], ACT.Sqrt).then_inc(degree_root, 1)

            def root(n, which, ready, done):
                act.wait_ge(ready, n + 1)
                nc.scalar.activation(std[:, which, :], mean_var[:, which, :, 1], ACT.Sqrt).then_inc(done, 1)

            def normalise1(n, par):
                act.wait_ge(norm1_ready, n + 1)
                for t in range(G):
                    nc.scalar.activation(xn[:, par, t, :], xg[:, par, t, :], ACT.Identity,
                                         bias=shift[:, 0, t:t + 1], scale=inv_std[:, 0, t:t + 1]
                                         ).then_inc(xn_ready, 1)

            root(0, 0, stats1_ready, std1_ready)
            act.wait_ge(x_loaded[0], 16)
            normalise1(0, 0)

            def step(n, par):
                last = isinstance(n, int) and n == NG
                if not (isinstance(n, int) and n >= NG - 1):
                    root(n + 1, 0, stats1_ready, std1_ready)
                if not last:
                    for t in range(G):
                        act.wait_ge(z_ready, n * G + t + 1)
                        if not (is_first(n) and t < 2):
                            act.wait_ge(gnn_ready, n * G + t - 1)
                        nc.scalar.copy(zt[:, t % 2, :], bank[t % 2][:, 0:D]).then_inc(zt_ready, 1)
                    root(n, 1, stats2_ready, std2_ready)
                if not is_first(n):
                    for t in range(G):
                        act.wait_ge(turned2, (n - 1) * G + t + 1)
                        if not (is_first(n, 2) and t < 2):
                            act.wait_ge(logits_ready, (n - 1) * G + t - 1)
                        nc.scalar.copy(xn2t[:, t % 2, :], bank[4 + t % 2][:, 0:D]).then_inc(xn2t_ready, 1)
                if not (isinstance(n, int) and n >= NG - 1):
                    normalise1(n + 1, 1 - par)
                if not last:
                    act.wait_ge(norm2_ready, n + 1)
                    if not is_first(n, 2):
                        act.wait_ge(low_ready, (n - 1) * G)
                        act.wait_ge(scattered[par], (n - par) * (8 * TOP * G))
                    for t in range(G):
                        nc.scalar.activation(xn2[:, par, t, :], h1[:, par, t, :], ACT.Identity,
                                             bias=shift[:, 1, t:t + 1], scale=inv_std[:, 1, t:t + 1]
                                             ).then_inc(xn2_ready, 1)
                    for t in range(G):
                        act.wait_ge(xn2_ready, n * G + t + 1)
                        nc.scalar.copy(rows16[:, par, t, 0:D], xn2[:, par, t, :]).then_inc(high_ready, 1)
                    if in_second_half[0]:
                        cut_weights(n)

            def cut_weights(n):
                e = n - NG // 2
                act.wait_ge(w_low, e + 1)
                for j in range(3):
                    nc.scalar.activation(halves[:, bass.ds(e * (2 * SLOT) + j * 2 * PIECE, PIECE)],
                                         weights[:, bass.ds((e + 1) * SLOT + j * PIECE, PIECE)],
                                         ACT.Identity, scale=w_scale[:, j:j + 1]).then_inc(w_high, 1)

            in_second_half = [False]

            def turn():
                in_second_half[0] = True

            phase1_steps(act, step, turn)

            def turn_x(i, par):
                act.wait_ge(x_turned, i + 1)
                nc.scalar.copy(xt[:, par, :, :, :].rearrange("p a c s -> p (a c s)"),
                               bank[6][:, :].bitcast(F16)).then_inc(xt_ready, 1)

            turn_x(0, 0)

            def tile(i, par):
                def high(hc):
                    act.wait_ge(hid_ready, i * HC + hc + 1)
                    nc.scalar.copy(hh[:, par, 0, hc, :], hid[:, hc, :]).then_inc(hid_high, 1)

                if not is_first(i, 2):
                    act.wait_ge(down_ready, i - 1)
                for hc in range(HC):
                    act.wait_ge(up_ready, i * HC + hc + 1)
                    if not (is_first(i) and hc < 2):
                        act.wait_ge(hid_ready, i * HC + hc - 1)
                    nc.scalar.activation(silu[:, hc % 2, :], bank[hc][:, 0:TILE], ACT.Silu,
                                         scale=silu_scale[:, 0:1]).then_inc(silu_ready, 1)
                    if hc >= 1:
                        high(hc - 1)
                high(HC - 1)
                if not (isinstance(i, int) and i == NT - 1):
                    turn_x(i + 1, 1 - par)
                act.wait_ge(margin_ready, i + 1)
                nc.scalar.activation(tanh[:, par, :], margin[:, par, :], ACT.Tanh, scale=0.5).then_inc(tanh_ready, 1)

            phase2_steps(act, tile)

        @block.vector
        def _(dve):
            steps = Steps(dve, dve_step)
            link, mark = steps.link, steps.mark

            dve.wait_ge(adj_loaded, 16)
            link(nc.vector.tensor_reduce(degree[:, 0:1], adj_sb[:, :], AX_X, ALU.add))
            nc.vector.tensor_scalar(degree[:, 1:2], degree[:, 0:1], 2.0 ** -126, None, ALU.max).then_inc(degree_sum, 1)
            mark(nc.vector.tensor_scalar(degree[:, 0:1], degree[:, 0:1], 0.0, None, ALU.is_gt))
            dve.wait_ge(degree_root, 1)
            link(nc.vector.reciprocal(degree[:, 3:4], degree[:, 2:3]))
            link(nc.vector.tensor_tensor(degree[:, 1:2], degree[:, 3:4], degree[:, 0:1], ALU.mult))
            nc.vector.tensor_scalar(adj_sb[:, :], adj_sb[:, :], degree[:, 1:2], None, ALU.mult
                                    ).then_inc(adj_half, 1)
            dve.wait_ge(gnn_loaded, 32)
            for j in range(2):
                link(nc.vector.tensor_copy(bias_cut[:, j, :], bias_row[:, j, :]))
                link(nc.vector.tensor_tensor(bias_row[:, j + 1, :], bias_row[:, j, :], bias_cut[:, j, :],
                                             ALU.subtract))
            nc.vector.tensor_copy(bias_cut[:, 2, :], bias_row[:, 2, :]).then_inc(bias_cut_ready, 1)
            dve.wait_ge(router_loaded, 32)
            nc.vector.tensor_scalar(wg_scaled[:, :, :], wg_sb[:, :, :], 1.0 / X_SCALE, None, ALU.mult)
            dve.wait_ge(adj_turned, 1)
            nc.vector.tensor_scalar(adj_t[:, :], bank[7][:, 0:P], degree[:, 1:2], None, ALU.mult
                                    ).then_inc(setup_ready, 1)

            def stats_of(src, which, ready):
                for t in range(G):
                    mark(nc.vector.bn_aggr(mean_var[:, which, t, :], stats[:, which, t, :]))
                steps.wait()
                nc.vector.tensor_scalar(mean_var[:, which, :, 1], mean_var[:, which, :, 1], EPS, None, ALU.add
                                        ).then_inc(ready, 1)

            def statistics1(n, par):
                dve.wait_ge(x_loaded[par], ((n - par) * 8) + 16)
                for t in range(G):
                    mark(nc.vector.bn_stats(stats[:, 0, t, :], xg[:, par, t, :]))
                steps.wait()
                dve.sem_inc(dve_passed)
                stats_of(xg, 0, stats1_ready)

            def inverse(n, which, std_ready, ready, scale):
                dve.wait_ge(std_ready, n + 1)
                link(nc.vector.reciprocal(inv_std[:, which, :], std[:, which, :]))
                if scale != 1.0:
                    link(nc.vector.tensor_scalar(inv_std[:, which, :], inv_std[:, which, :], scale, None, ALU.mult))
                nc.vector.scalar_tensor_tensor(shift[:, which, :], mean_var[:, which, :, 0], -1.0,
                                               inv_std[:, which, :], ALU.mult, ALU.mult).then_inc(ready, 1)

            def residual(n, par):
                if not is_first(n, 2):
                    dve.wait_ge(h1_stored[par], (n - par) * 8)
                for t in range(G):
                    dve.wait_ge(gnn_ready, n * G + t + 1)
                    nc.vector.tensor_tensor(h1[:, par, t, :], bank[2 + t % 2][:, 0:D], xg[:, par, t, :], ALU.add
                                            ).then_inc(h1_done, 1)
                    if t >= 1:
                        dve.wait_ge(h1_done, n * G + t)
                        mark(nc.vector.bn_stats(stats[:, 1, t - 1, :], h1[:, par, t - 1, :]))
                dve.wait_ge(h1_done, n * G + G)
                mark(nc.vector.bn_stats(stats[:, 1, G - 1, :], h1[:, par, G - 1, :]))
                steps.wait()
                dve.sem_inc(dve_passed)
                stats_of(h1, 1, stats2_ready)

            def route(n, par):
                dve.wait_ge(logits_ready, (n + 1) * G)
                link_taken(n, nc.vector.tensor_tensor(
                    logits[:, :, :], bank[6][:, 0:G * E].rearrange("p (t e) -> p t e", t=G),
                    bg_sb[:, :].unsqueeze(1).to_broadcast([P, G, E]), ALU.add))
                for k in range(TOP):
                    src = (logits, rest)[k]
                    link(nc.vector.tensor_reduce(best[:, k, :], src[:, :, :], AX_X, ALU.max))
                    link(nc.vector.tensor_tensor(is_top[:, :, :], src[:, :, :],
                                                 best[:, k, :].unsqueeze(2).to_broadcast([P, G, E]), ALU.is_equal))
                    link(nc.vector.tensor_tensor(rank[:, :, :], is_top[:, :, :],
                                                 descending[:, :].unsqueeze(1).to_broadcast([P, G, E]), ALU.mult))
                    link(nc.vector.tensor_reduce(chosen[:, k, :], rank[:, :, :], AX_X, ALU.max))
                    link(nc.vector.tensor_tensor(onehot[:, k, :, :], rank[:, :, :],
                                                 chosen[:, k, :].unsqueeze(2).to_broadcast([P, G, E]), ALU.is_equal))
                    if k == 0:
                        link(nc.vector.scalar_tensor_tensor(rest[:, :, :], onehot[:, 0, :, :], -3.0e38,
                                                            logits[:, :, :], ALU.mult, ALU.add))
                link(nc.vector.tensor_tensor(picks[:, :, :], onehot[:, 0, :, :], onehot[:, 1, :, :], ALU.add))
                link(nc.vector.tensor_reduce(picks_sum[:, :], picks[:, :, :].rearrange("p t e -> p e t"),
                                             AX_X, ALU.add))
                if not is_first(n):
                    dve.wait_ge(picks_ready, n)
                nc.vector.tensor_tensor(running[:, 1 - par, :], running[:, par, :], picks_sum[:, :], ALU.add
                                        ).then_inc(picks_ready, 1)
                nc.vector.tensor_tensor(rows[:, par, :, MARGIN], best[:, 0, :], best[:, 1, :], ALU.subtract)
                nc.vector.tensor_scalar(rows[:, par, :, FIRST], chosen[:, 0, :], -1.0, float(E), ALU.mult, ALU.add)
                link(nc.vector.tensor_copy(rows[:, par, :, TOKEN].bitcast(I32), token[:, :]))
                mark(nc.vector.tensor_scalar(token[:, :], token[:, :], G * P, None, ALU.add))

            def link_taken(n, instruction):
                instruction.then_inc(logits_taken, 1)
                dve.wait_ge(logits_taken, n + 1)

            def low_parts(n, par):
                for t in range(G):
                    dve.wait_ge(high_ready, n * G + t + 1)
                    nc.vector.tensor_tensor(rows16[:, par, t, D:2 * D], xn2[:, par, t, :], rows16[:, par, t, 0:D],
                                            ALU.subtract).then_inc(low_ready, 1)

            def places(n, par):
                dve.wait_ge(before_ready, n + 1)
                link(nc.vector.tensor_tensor(place[:, :, :], bank[7][:, 0:G * E].rearrange("p (t e) -> p t e", t=G),
                                             region_of[:, :].unsqueeze(1).to_broadcast([P, G, E]), ALU.add))
                for k in range(TOP):
                    mark(nc.vector.tensor_tensor(place_of[:, k, :, :], onehot[:, k, :, :], place[:, :, :], ALU.mult))
                steps.wait()
                link(nc.vector.tensor_reduce(slot_of[:, :, :], place_of[:, :, :, :], AX_X, ALU.add))
                if not is_first(n, 2):
                    dve.wait_ge(scattered[par], (n - par) * (8 * TOP * G))
                nc.vector.tensor_copy(slot_index[:, par, :, :], slot_of[:, :, :]).then_inc(places_ready, 1)

            dve.wait_ge(consts_ready, 1)
            statistics1(0, 0)
            inverse(0, 0, std1_ready, norm1_ready, 1.0)

            def step(n, par):
                last = isinstance(n, int) and n == NG
                if not (isinstance(n, int) and n >= NG - 1):
                    statistics1(n + 1, 1 - par)
                if not last:
                    residual(n, par)
                if not (isinstance(n, int) and n >= NG - 1):
                    inverse(n + 1, 0, std1_ready, norm1_ready, 1.0)
                if not last:
                    inverse(n, 1, std2_ready, norm2_ready, X_SCALE)
                    if not in_second_half[0]:
                        dve.wait_ge(w_loaded[par], (n - par) * 24 + 48)
                        nc.vector.tensor_reduce(
                            w_max[:, bass.ds(n, 1), :].rearrange("p e j -> p (e j)"),
                            weights[:, bass.ds((n + 1) * SLOT, SLOT)].rearrange("p (j k) -> p j k", j=3),
                            AX_X, ALU.max, apply_absolute_value=True).then_inc(max_step, 1)
                if not is_first(n):
                    route(n - 1, 1 - par)
                if not last:
                    low_parts(n, par)
                if not is_first(n):
                    places(n - 1, 1 - par)
                if not last and in_second_half[0]:
                    e = n - NG // 2
                    for j in range(3):
                        dve.wait_ge(w_high, e * 3 + j + 1)
                        low = nc.vector.scalar_tensor_tensor(
                            halves[:, bass.ds(e * (2 * SLOT) + (2 * j + 1) * PIECE, PIECE)],
                            weights[:, bass.ds((e + 1) * SLOT + j * PIECE, PIECE)], w_scale[:, j:j + 1],
                            halves[:, bass.ds(e * (2 * SLOT) + 2 * j * PIECE, PIECE)], ALU.mult, ALU.subtract)
                    low.then_inc(w_low, 1)

            in_second_half = [False]

            def scales():
                in_second_half[0] = True
                one = Steps(dve, scale_step)
                dve.wait_ge(max_step, E)
                nc.vector.tensor_reduce(w_top[:, :], w_max[:, :, :].rearrange("p e j -> p j e"), AX_X, ALU.max
                                        ).then_inc(max_ready, 1)
                dve.wait_ge(max_all, 1)
                one.link(nc.vector.tensor_scalar(w_top[:, :], w_top_all[:, :], 2.0 ** -30, None, ALU.max))
                one.link(nc.vector.tensor_scalar(w_low2[:, :].bitcast(I32), w_top[:, :].bitcast(I32),
                                                 0x7F800000, None, ALU.bitwise_and))
                one.link(nc.vector.tensor_scalar(w_inv2[:, :].bitcast(I32), w_low2[:, :].bitcast(I32),
                                                 0x7F800000, None, ALU.bitwise_xor))
                nc.vector.tensor_scalar(w_scale[:, :], w_inv2[:, :], 2.0 ** 12, None, ALU.mult)
                nc.vector.tensor_scalar(silu_scale[:, :], w_low2[:, 0:1], 2.0 ** -13 / X_SCALE, None, ALU.mult)
                nc.vector.tensor_scalar(up_scale[:, :], w_inv2[:, 0:1], 2.0 ** -17 / X_SCALE, None, ALU.mult)
                one.link(nc.vector.tensor_tensor(y_scale[:, :], w_low2[:, 0:1], w_low2[:, 1:2], ALU.mult))
                nc.vector.scalar_tensor_tensor(y_scale[:, :], w_low2[:, 2:3], 2.0 ** -11, y_scale[:, :],
                                               ALU.mult, ALU.mult).then_inc(scales_ready, 1)
                dve.wait_ge(scales_ready, 1)
                dve.sem_inc(w_low)

            phase1_steps(dve, step, scales, steps, DVE_LINKS)

            table = Steps(dve, table_step)
            dve.wait_ge(counts_ready, 1)
            table.link(nc.vector.tensor_copy(count[:, :], bank[6][:, 0:E]))
            table.link(nc.vector.tensor_tensor(tile_tmp[:, 0, 0:E], count[:, :], region_of[:, :], ALU.add))
            nc.vector.tensor_copy(pad_at[:, :], tile_tmp[:, 0, 0:E]).then_inc(pad_at_ready, 1)
            table.link(nc.vector.tensor_scalar(tiles_i[:, 0, :], count[:, :], float(TILE - 1), None, ALU.add))
            table.link(nc.vector.tensor_scalar(tiles_i[:, 1, :], tiles_i[:, 0, :], TILE.bit_length() - 1, None,
                                               ALU.logical_shift_right))
            table.link(nc.vector.tensor_copy(tiles[:, :], tiles_i[:, 1, :]))
            table.link(nc.vector.tensor_tensor(upto[:, :, :], up_to[:, :, :],
                                               tiles[:, :].unsqueeze(1).to_broadcast([P, E, E]), ALU.mult))
            table.link(nc.vector.tensor_reduce(tiles_end[:, :], upto[:, :, :], AX_X, ALU.add))
            table.link(nc.vector.tensor_tensor(past[:, :, :], tile_no[:, :].unsqueeze(2).to_broadcast([P, NTP, E]),
                                               tiles_end[:, :].unsqueeze(1).to_broadcast([P, NTP, E]), ALU.is_ge))
            table.mark(nc.vector.tensor_reduce(tile_expert[:, :], past[:, :, :], AX_X, ALU.add))
            table.link(nc.vector.tensor_tensor(past_tiles[:, :, :], past[:, :, :],
                                               tiles[:, :].unsqueeze(1).to_broadcast([P, NTP, E]), ALU.mult))
            table.link(nc.vector.tensor_reduce(tile_start[:, :], past_tiles[:, :, :], AX_X, ALU.add))
            table.mark(nc.vector.tensor_tensor(tile_tmp[:, 0, :], tile_no[:, :], tile_start[:, :], ALU.subtract))
            table.link(nc.vector.tensor_scalar(tile_tmp[:, 1, :], tile_expert[:, :], float(E), float(TILE),
                                               ALU.is_lt, ALU.mult))
            table.link(nc.vector.tensor_tensor(tile_tmp[:, 2, :], tile_tmp[:, 0, :], tile_tmp[:, 1, :], ALU.mult))
            nc.vector.scalar_tensor_tensor(tile_row[:, :], tile_expert[:, :], float(REGION), tile_tmp[:, 2, :],
                                           ALU.mult, ALU.add)
            nc.vector.tensor_scalar(tile_weights[:, :], tile_expert[:, :], float(E - 1), float(2 * SLOT),
                                    ALU.min, ALU.mult).then_inc(tiles_ready, 1)
            dve.wait_ge(tiles_ready, 1)

            def read_meta(i, par):
                dve.wait_ge(rows_loaded[par], (i - par) * 8 + 16)
                if not is_first(i, 2):
                    dve.wait_ge(y_added, (i - 1) * 32)
                nc.vector.tensor_copy(target[:, par, :], xr[:, par, :, TOKEN].bitcast(I32))
                nc.vector.tensor_scalar(own[:, par, :], xr[:, par, :, FIRST], tile_expert[:, bass.ds(i, 1)], 2.0,
                                        ALU.is_equal, ALU.mult).then_inc(own_ready, 1)
                dve.wait_ge(own_ready, i + 1)
                nc.vector.scalar_tensor_tensor(margin[:, par, :], own[:, par, :], 1.0, xr[:, par, :, MARGIN],
                                               ALU.subtract, ALU.mult).then_inc(margin_ready, 1)

            def tile(i, par):
                def low(hc):
                    dve.wait_ge(hid_high, i * HC + hc + 1)
                    nc.vector.tensor_tensor(hh[:, par, 1, hc, :], hid[:, hc, :], hh[:, par, 0, hc, :],
                                            ALU.subtract).then_inc(hid_low, 1)

                for hc in range(HC):
                    dve.wait_ge(silu_ready, i * HC + hc + 1)
                    if not is_first(i):
                        dve.wait_ge(hid_low, (i - 1) * HC + hc + 1)
                    nc.vector.scalar_tensor_tensor(hid[:, hc, :], bank[hc][:, TILE:2 * TILE], up_scale[:, 0:1],
                                                   silu[:, hc % 2, :], ALU.mult, ALU.mult).then_inc(hid_ready, 1)
                    if hc >= 1:
                        low(hc - 1)
                low(HC - 1)
                read_meta(i, par)
                if not is_first(i):
                    scale_y(i - 1, 1 - par)
                dve.wait_ge(tanh_ready, i + 1)
                nc.vector.tensor_scalar(gate[:, par, :], tanh[:, par, :], 1.0, y_scale[:, 0:1], ALU.add, ALU.mult
                                        ).then_inc(gate_ready, 1)

            def scale_y(i, par):
                dve.wait_ge(gate_ready, i + 1)
                dve.wait_ge(down_ready, i + 1)
                for c in range(2):
                    last = nc.vector.tensor_scalar(y[:, par, c, :], bank[DOWN[par]][:, c * D:(c + 1) * D],
                                                   gate[:, par, c:c + 1], None, ALU.mult)
                last.then_inc(y_ready, 1)

            phase2_steps(dve, tile)
            scale_y(NT - 1, 0)

        @block.tensor
        def _(pe):
            pe.wait_ge(consts_ready, 1)
            pe.wait_ge(adj_half, 1)
            nc.tensor.transpose(bank[7][:, 0:P], adj_sb[:, :], ident32[:, :]).then_inc(adj_turned, 1)
            pe.wait_ge(setup_ready, 1)
            pe.wait_ge(bias_moved, 48)

            def step(n, par):
                last = isinstance(n, int) and n == NG

                def z(t):
                    pe.wait_ge(xn_ready, n * G + t + 1)
                    for c in range(KC):
                        mm = nc.tensor.matmul(bank[t % 2][:, c * P:(c + 1) * P], xn[:, par, t, c * P:(c + 1) * P],
                                              adj_t[:, :], start=True, stop=True)
                    mm.then_inc(z_ready, 1)

                def gnn(t):
                    pe.wait_ge(zt_ready, n * G + t + 1)
                    if not (is_first(n) and t < 2):
                        pe.wait_ge(h1_done, n * G + t - 1)
                    o = bank[2 + t % 2][:, 0:D]
                    nc.tensor.matmul(o, ones[0:3, :], bias3[:, :], start=True, stop=False)
                    for c in range(KC):
                        mm = nc.tensor.matmul(o, zt[:, t % 2, c * P:(c + 1) * P], gw_sb[:, c, :],
                                              start=False, stop=(c == KC - 1))
                    mm.then_inc(gnn_ready, 1)

                def turn2(t):
                    pe.wait_ge(xn2_ready, (n - 1) * G + t + 1)
                    for c in range(KC):
                        mm = nc.tensor.transpose(bank[4 + t % 2][:, c * P:(c + 1) * P],
                                                 xn2[:, 1 - par, t, c * P:(c + 1) * P], ident32[:, :])
                    mm.then_inc(turned2, 1)

                def router(t):
                    pe.wait_ge(xn2t_ready, (n - 1) * G + t + 1)
                    if t == 0 and not is_first(n, 2):
                        pe.wait_ge(logits_taken, n - 1)
                    for c in range(KC):
                        mm = nc.tensor.matmul(bank[6][:, t * E:(t + 1) * E], xn2t[:, t % 2, c * P:(c + 1) * P],
                                              wg_scaled[:, c, :], start=(c == 0), stop=(c == KC - 1))
                    mm.then_inc(logits_ready, 1)

                if not last:
                    z(0)
                    for t in range(G):
                        if t + 1 < G:
                            z(t + 1)
                        gnn(t)
                if not is_first(n):
                    turn2(0)
                    for t in range(G):
                        if t + 1 < G:
                            turn2(t + 1)
                        router(t)
                    pe.wait_ge(picks_ready, n)
                    if not is_first(n, 2):
                        pe.wait_ge(places_ready, n - 1)
                    flat = picks[:, :, :].rearrange("p t e -> p (t e)")
                    o = bank[7]
                    nc.tensor.matmul(o[:, 0:G * E], before[:, :], flat, start=True, stop=False)
                    for t in range(G - 1):
                        nc.tensor.matmul(o[:, (t + 1) * E:G * E], ones[:, :],
                                         picks[:, t, :].unsqueeze(1).to_broadcast([P, G - 1 - t, E]),
                                         start=False, stop=False)
                    mm = nc.tensor.matmul(o[:, 0:G * E], ones[:, :],
                                          running[:, 1 - par, :].unsqueeze(1).to_broadcast([P, G, E]),
                                          start=False, stop=True)
                    mm.then_inc(before_ready, 1)

            phase1_steps(pe, step, lambda: None)
            nc.tensor.matmul(bank[6][:, 0:E], ones[:, :], running[:, NG % 2, :], start=True, stop=True
                             ).then_inc(counts_ready, 1)

            def turn_x(i, par):
                pe.wait_ge(rows_loaded[par], (i - par) * 8 + 16)
                if not is_first(i):
                    pe.wait_ge(xt_ready, i)
                o = bank[6][:, :].bitcast(F16)
                for c in range(2):
                    for part in range(2):
                        for k in range(KC):
                            at = (part * KC + k) * TILE + c * P
                            mm = nc.tensor.transpose(o[:, at:at + P],
                                                     xr16[:, par, c, part * D + k * P:part * D + (k + 1) * P],
                                                     ident16[:, :])
                mm.then_inc(x_turned, 1)

            def down(i, par):
                w = pe.value_load(tile_weights[0:1, bass.ds(i, 1)], min_val=0, max_val=(E - 1) * 2 * SLOT)
                pe.wait_ge(hid_low, (i + 1) * HC)
                if not is_first(i, 2):
                    pe.wait_ge(y_ready, i - 1)
                for c in range(2):
                    terms = [(hc, a, b) for hc in range(HC) for a, b in ((0, 0), (0, 1), (1, 0))]
                    for j, (hc, a, b) in enumerate(terms):
                        mm = nc.tensor.matmul(bank[DOWN[par]][:, c * D:(c + 1) * D],
                                              hh[:, par, a, hc, c * P:(c + 1) * P],
                                              halves[:, bass.ds(w + ((4 + b) * PIECE + hc * D), D)],
                                              start=(j == 0), stop=(j == len(terms) - 1))
                mm.then_inc(down_ready, 1)

            pe.wait_ge(tiles_ready, 1)
            pe.wait_ge(w_low, E + 1)
            turn_x(0, 0)

            def tile(i, par):
                w = pe.value_load(tile_weights[0:1, bass.ds(i, 1)], min_val=0, max_val=(E - 1) * 2 * SLOT)
                pe.wait_ge(xt_ready, i + 1)
                for hc in range(HC):
                    if not is_first(i):
                        pe.wait_ge(hid_ready, (i - 1) * HC + hc + 1)
                    for side in range(2):
                        terms = [(k, a, b) for k in range(KC) for a, b in ((0, 0), (0, 1), (1, 0))]
                        for j, (k, a, b) in enumerate(terms):
                            mm = nc.tensor.matmul(
                                bank[hc][:, side * TILE:(side + 1) * TILE],
                                halves[:, bass.ds(w + ((2 * side + a) * PIECE + k * HID + hc * P), P)],
                                xt[:, par, b, k, :], start=(j == 0), stop=(j == len(terms) - 1))
                    mm.then_inc(up_ready, 1)
                if not (isinstance(i, int) and i == NT - 1):
                    turn_x(i + 1, 1 - par)
                if not is_first(i):
                    down(i - 1, 1 - par)

            phase2_steps(pe, tile)
            down(NT - 1, 0)


_INS = ["x", "adj", "L0_gnn_weight", "L0_gnn_bias", "L0_ffn_Wg", "L0_ffn_bg", "L0_ffn_W1", "L0_ffn_W3", "L0_ffn_W2"]
PAD_ROWS = 2 * P


def kernel(**inputs):
    import numpy as _np
    import concourse.bacc as _bacc
    from concourse import mybir as _mybir
    from concourse.bass_utils import run_bass_kernel_spmd as _run

    nc = _bacc.Bacc("TRN2", target_bir_lowering=False, num_devices=1)
    arrays, args = {}, []
    for name in _INS:
        a = _np.ascontiguousarray(inputs[name])
        arrays[f"in_{name}_dram"] = a
        args.append(nc.dram_tensor(f"in_{name}_dram", a.shape, _mybir.dt.from_np(a.dtype), kind="ExternalInput").ap())
    b, n, d = inputs["x"].shape
    out = nc.dram_tensor("out_0_dram", (b * n + PAD_ROWS, d), F32, kind="ExternalOutput").ap()
    build(nc, *args, out)
    r = _run(nc, [arrays], core_ids=[0])
    return r.results[0]["out_0_dram"][:b * n].reshape(b, n, d)
```

```python
from contextlib import ExitStack

import concourse.bass as bass
from concourse import mybir

ALU = mybir.AluOpType
ACT = mybir.ActivationFunctionType
F32 = mybir.dt.float32
F16 = mybir.dt.float16
BF16 = mybir.dt.bfloat16
I32 = mybir.dt.int32
U32 = mybir.dt.uint32
AX_X = mybir.AxisListType.X
MAX_OVER_PARTITIONS = bass.bass_isa.ReduceOp.max

P = 128
EPS = 1e-5


class Steps:

    def __init__(self, engine, semaphore):
        self.engine, self.semaphore, self.at, self.done = engine, semaphore, 0, 0

    def mark(self, instruction):
        instruction.then_inc(self.semaphore, 1)
        self.done += 1

    def wait(self):
        self.engine.wait_ge(self.semaphore, self.at + self.done)

    def link(self, instruction):
        self.mark(instruction)
        self.wait()

    def restart(self, at):
        self.at, self.done = at, 0


def build(nc, x, adj, gnn_w, gnn_b, wg, bg, w1, w3, w2, out):
    B, N, D = x.shape
    E, _, HID = w1.shape
    T = B * N
    TOP = 2
    assert N == P and D == 2 * P and HID == 4 * P and T % (4 * P) == 0
    KC = D // P
    HC = HID // P
    G = 4
    NG = T // (G * P)
    TILE = 2 * P
    NT = T * TOP // TILE + E - 1
    NTP = NT + 1
    REGION = T + TILE
    ROW = D + 8
    TOKEN, MARGIN, FIRST = D, D + 1, D + 2
    PIECE = KC * HID
    SLOT = 3 * PIECE
    PER_GROUP = G * P * TOP // TILE
    LEAD = 8
    ROUTED = LEAD - 1
    EARLY = ROUTED * PER_GROUP - (E - 1)
    PER_STEP = 3
    SQUARES, CUTS = 4, 4
    PAIR = 2
    FIRST_CUT = SQUARES + 1
    assert HC * D == PIECE and PAIR * SQUARES == E and PAIR * CUTS == E and FIRST_CUT + CUTS == LEAD + 1
    INTERLEAVED = PER_STEP * (NG - 2 - LEAD)
    assert (NG - LEAD) % 2 == 0 and INTERLEAVED < EARLY and (NT - EARLY) % 2 == 0
    X_SCALE = 2.0 ** 11
    DVE_LINKS = {"cut": 36, "tiles": 36}
    ROUTER = 4
    DOWN = (5, 7)
    TURN = 6
    SUM = 7

    tokens_in = x.rearrange("b n d -> (b n) d")
    routed = nc.dram_tensor("routed", (E * REGION + TILE, ROW), F32).ap()

    with ExitStack() as ctx:
        def sb(name, shape, dt):
            return ctx.enter_context(nc.sbuf_tensor(name, shape, dt))

        def sem(name):
            return ctx.enter_context(nc.semaphore(name))

        bank = [ctx.enter_context(nc.psum_tensor(f"bank{i}", [P, 512], F32)) for i in range(8)]

        ident32 = sb("ident32", [P, P], F32)
        ident16 = sb("ident16", [P, P], F16)
        before = sb("before", [P, P], BF16)
        ones = sb("ones", [P, P], BF16)
        up_to = sb("up_to", [P, E, E], F32)
        expert_no = sb("expert_no", [P, E], F32)
        region_of = sb("region_of", [P, E], F32)
        tile_no = sb("tile_no", [P, NTP], F32)
        adj_sb = sb("adj_sb", [P, P], F32)
        adj_t = sb("adj_t", [P, P], F32)
        degree = sb("degree", [P, 4], F32)
        gw_sb = sb("gw_sb", [P, KC, D], F32)
        bias_row = sb("bias_row", [1, 3, D], F32)
        bias_cut = sb("bias_cut", [1, 3, D], BF16)
        bias3 = sb("bias3", [3, D], BF16)
        wg_sb = sb("wg_sb", [P, KC, E], F32)
        wg_scaled = sb("wg_scaled", [P, KC, E], F32)
        bg_sb = sb("bg_sb", [P, E], F32)
        weights = sb("weights", [P, (E + 1) * SLOT], F32)
        halves = weights[:, :].bitcast(F16)
        shared = sb("shared", [P, 3 * HC * TILE], F32)
        squares = shared[:, :].bitcast(BF16).rearrange("p (k w) -> p k w", k=PAIR)
        assert PAIR * SLOT == 6 * HC * TILE
        norm = sb("norm", [P, 4], F32)
        low2 = sb("low2", [P, 1], F32)
        inv2 = sb("inv2", [P, 1], F32)
        cube2 = sb("cube2", [P, 1], F32)
        w_scale = sb("w_scale", [P, 1], F32)
        silu_scale = sb("silu_scale", [P, 1], F32)
        up_scale = sb("up_scale", [P, 1], F32)
        y_scale = sb("y_scale", [P, 1], F32)
        xg = sb("xg", [P, 2, G, D], F32)
        xn = sb("xn", [P, 2, G, D], F32)
        zt = sb("zt", [P, 2, D], F32)
        h1 = sb("h1", [P, 2, G, D], F32)
        xn2 = sb("xn2", [P, 2, G, D], F32)
        xn2t = sb("xn2t", [P, 2, D], F32)
        rows = sb("rows", [P, 2, G, ROW], F32)
        rows16 = rows[:, :, :, :].bitcast(F16)
        stats = sb("stats", [P, 2, G, 6], F32)
        mean_var = sb("mean_var", [P, 2, G, 2], F32)
        std = sb("std", [P, 2, G], F32)
        inv_std = sb("inv_std", [P, 2, G], F32)
        shift = sb("shift", [P, 2, G], F32)
        logits = sb("logits", [P, G, E], F32)
        top8 = sb("top8", [P, G, 8], F32)
        top_index = sb("top_index", [P, G, 8], U32)
        onehot = sb("onehot", [P, TOP, G, E], F32)
        picks = sb("picks", [P, G, E], BF16)
        picks_sum = sb("picks_sum", [P, E], F32)
        running = sb("running", [P, 2, E], BF16)
        token = sb("token", [P, G], I32)
        place = sb("place", [P, G, E], F32)
        place_of = sb("place_of", [P, TOP, G, E], F32)
        slot_of = sb("slot_of", [P, TOP, G], F32)
        slot_index = sb("slot_index", [P, 2, TOP, G], U32)
        pad_rows = sb("pad_rows", [P, 2, ROW], F32)
        count = sb("count", [P, E], F32)
        count_i = sb("count_i", [P, 2, E], I32)
        full = sb("full", [P, E], F32)
        first = sb("first", [P, E + 1], F32)
        whole = sb("whole", [P, E], F32)
        left = sb("left", [P, E], F32)
        coef = sb("coef", [P, E], F32)
        upto = sb("upto", [P, E, E], F32)
        ends = sb("ends", [P, E], F32)
        past = sb("past", [P, NTP, E], F32)
        past_coef = sb("past_coef", [P, NTP, E], F32)
        tile_expert = sb("tile_expert", [P, NTP], F32)
        tile_tmp = sb("tile_tmp", [P, 4, NTP], F32)
        expert_tmp = sb("expert_tmp", [P, 2, E], F32)
        tile_row = sb("tile_row", [P, NTP], I32)
        tile_weights = sb("tile_weights", [P, NTP], I32)
        pad_at = sb("pad_at", [P, E], I32)
        xr = sb("xr", [P, 2, 2, ROW], F32)
        xr16 = xr[:, :, :, :].bitcast(F16)
        xt = sb("xt", [P, 2, 2, KC, TILE], F16)
        silu = sb("silu", [P, 2, TILE], F32)
        hid = shared[:, 0:HC * TILE].rearrange("p (c s) -> p c s", c=HC)
        hh = shared[:, HC * TILE:].bitcast(F16).rearrange("p (i a c s) -> p i a c s", i=2, a=2, c=HC)
        y = sb("y", [P, 2, 2, D], F32)
        target = sb("target", [P, 2, 2], U32)
        own = sb("own", [P, 2, 2], F32)
        margin = sb("margin", [P, 2, 2], F32)
        tanh = sb("tanh", [P, 2, 2], F32)
        gate = sb("gate", [P, 2, 2], F32)

        adj_loaded = sem("adj_loaded")
        gnn_loaded = sem("gnn_loaded")
        router_loaded = sem("router_loaded")
        bias_moved = sem("bias_moved")
        x_loaded = [sem(f"x_loaded{i}") for i in range(2)]
        w_loaded = [sem(f"w_loaded{i}") for i in range(SQUARES)]
        h1_stored = [sem(f"h1_stored{i}") for i in range(2)]
        dump_stored = sem("dump_stored")
        blank_stored = sem("blank_stored")
        pads_stored = sem("pads_stored")
        scattered = [sem(f"scattered{i}") for i in range(2)]
        rows_loaded = [sem(f"rows_loaded{i}") for i in range(2)]
        y_added = sem("y_added")
        pool_passed = sem("pool_passed")
        dve_passed = sem("dve_passed")
        pool_step = sem("pool_step")
        dve_step = sem("dve_step")
        consts_ready = sem("consts_ready")
        degree_sum = sem("degree_sum")
        degree_root = sem("degree_root")
        adj_half = sem("adj_half")
        adj_turned = sem("adj_turned")
        bias_cut_ready = sem("bias_cut_ready")
        setup_ready = sem("setup_ready")
        stats1_ready = sem("stats1_ready")
        std1_ready = sem("std1_ready")
        norm1_ready = sem("norm1_ready")
        xn_ready = sem("xn_ready")
        z_ready = sem("z_ready")
        zt_ready = sem("zt_ready")
        gnn_ready = sem("gnn_ready")
        h1_done = sem("h1_done")
        stats2_ready = sem("stats2_ready")
        std2_ready = sem("std2_ready")
        norm2_ready = sem("norm2_ready")
        xn2_ready = sem("xn2_ready")
        high_ready = sem("high_ready")
        low_ready = sem("low_ready")
        turned2 = sem("turned2")
        xn2t_ready = sem("xn2t_ready")
        logits_ready = sem("logits_ready")
        logits_taken = sem("logits_taken")
        picks_ready = sem("picks_ready")
        before_ready = sem("before_ready")
        places_ready = sem("places_ready")
        squares_act = sem("squares_act")
        squares_dve = sem("squares_dve")
        squares_summed = sem("squares_summed")
        norm_ready = sem("norm_ready")
        root_ready = sem("root_ready")
        running_ready = sem("running_ready")
        scales_ready = sem("scales_ready")
        w_high = sem("w_high")
        w_low = sem("w_low")
        counts_ready = sem("counts_ready")
        pad_at_ready = sem("pad_at_ready")
        tiles_ready = sem("tiles_ready")
        x_turned = sem("x_turned")
        xt_ready = sem("xt_ready")
        own_ready = sem("own_ready")
        gate_ready = sem("gate_ready")
        scale_step = sem("scale_step")
        table_step = sem("table_step")
        sum_taken = sem("sum_taken")
        margin_ready = sem("margin_ready")
        tanh_ready = sem("tanh_ready")
        up_ready = sem("up_ready")
        silu_ready = sem("silu_ready")
        hid_ready = sem("hid_ready")
        hid_high = sem("hid_high")
        hid_low = sem("hid_low")
        down_ready = sem("down_ready")
        y_ready = sem("y_ready")

        def phase1_steps(engine, step, between, steps=None):
            def pairs(n0, n1, kind):
                base = steps.at + steps.done if steps is not None else 0
                with engine.Fori(0, (n1 - n0) // 2) as i:
                    for k in range(2):
                        if steps is not None:
                            steps.restart(i * (2 * DVE_LINKS[kind]) + (base + k * DVE_LINKS[kind]))
                        step(i * 2 + (n0 + k), (n0 + k) % 2, kind)
                        assert steps is None or steps.done == DVE_LINKS[kind], (kind, steps.done)
                if steps is not None:
                    steps.restart(base + (n1 - n0) * DVE_LINKS[kind])

            for n in range(SQUARES):
                step(n, n % 2, "squares")
            step(SQUARES, SQUARES % 2, "scales")
            pairs(FIRST_CUT, LEAD + 1, "cut")
            between()
            step(LEAD + 1, (LEAD + 1) % 2, "tiles")
            pairs(LEAD + 2, NG - 2, "tiles")
            step(NG - 2, (NG - 2) % 2, "tiles")
            step(NG - 1, (NG - 1) % 2, "last")
            step(NG, NG % 2, "end")

        def early(n, par, k):
            return (n - (LEAD + 1)) * PER_STEP + k, ((par - (LEAD + 1)) * PER_STEP + k) % 2

        def tiles_after(engine, tile, after_first, late=lambda: None):
            for i in range(INTERLEAVED, EARLY):
                tile(i, i % 2)
                if i == INTERLEAVED:
                    after_first()
            late()
            with engine.Fori(0, (NT - EARLY) // 2 - 1) as i:
                for k in range(2):
                    tile(i * 2 + (EARLY + k), (EARLY + k) % 2)
            tile(NT - 2, (NT - 2) % 2)
            tile(NT - 1, (NT - 1) % 2)

        def is_first(n, k=1):
            return isinstance(n, int) and n < k

        block = ctx.enter_context(nc.Block())

        @block.sync
        def _(sp):
            sp.dma_start(adj_sb[:, :], adj).then_inc(adj_loaded, 16)
            sp.dma_start(xg[:, 0, :, :], tokens_in[0:G * P, :].rearrange("(t p) d -> p t d", p=P)
                         ).then_inc(x_loaded[0], 16)
            sp.dma_start(gw_sb[:, :, :], gnn_w.rearrange("(c p) d -> p c d", p=P)).then_inc(gnn_loaded, 16)
            sp.dma_start(bias_row[:, 0, :], gnn_b.rearrange("(a d) -> a d", a=1)).then_inc(gnn_loaded, 16)
            sp.dma_start(wg_sb[:, :, :], wg.rearrange("(c p) e -> p c e", p=P)).then_inc(router_loaded, 16)
            sp.dma_start(bg_sb[:, :], bg.partition_broadcast(P)).then_inc(router_loaded, 16)
            sp.dma_start(xg[:, 1, :, :], tokens_in[G * P:2 * G * P, :].rearrange("(t p) d -> p t d", p=P)
                         ).then_inc(x_loaded[1], 16)
            sp.wait_ge(bias_cut_ready, 1)
            for j in range(3):
                sp.dma_start(bias3[j:j + 1, :], bias_cut[:, j, :]).then_inc(bias_moved, 16)

            def load_weights(n):
                for e in range(n * PAIR, (n + 1) * PAIR):
                    for j, (w, c) in enumerate(((w1, KC), (w3, KC), (w2, HC))):
                        at = (e + 1) * SLOT + j * PIECE
                        sp.dma_start(weights[:, at:at + PIECE].rearrange("p (c h) -> p c h", c=c),
                                     w[e].rearrange("(c p) h -> p c h", p=P)).then_inc(w_loaded[n], 16)

            def load_tile(i, par):
                if not is_first(i, 2):
                    sp.wait_ge(x_turned, i - 1)
                    sp.wait_ge(margin_ready, i - 1)
                at = sp.value_load(tile_row[0:1, bass.ds(i, 1)], min_val=0, max_val=E * REGION)
                sp.dma_start(xr[:, par, :, :],
                             routed[bass.ds(at, TILE), :].rearrange("(c p) w -> p c w", p=P)
                             ).then_inc(rows_loaded[par], 16)

            def step(n, par, kind):
                if kind == "squares":
                    load_weights(n)
                if kind != "end":
                    sp.wait_ge(h1_done, (n + 1) * G)
                    sp.dma_start(out[bass.ds(n * (G * P), G * P), :].rearrange("(t p) d -> p t d", p=P),
                                 h1[:, par, :, :]).then_inc(h1_stored[par], 16)
                    if not (isinstance(n, int) and n + 2 >= NG):
                        sp.dma_start(xg[:, par, :, :], tokens_in[bass.ds((n + 2) * (G * P), G * P), :].rearrange(
                            "(t p) d -> p t d", p=P)).then_inc(x_loaded[par], 16)
                if kind == "tiles":
                    for k in range(PER_STEP):
                        i, tile_par = early(n, par, k)
                        load_tile(i + 2, tile_par)

            def first_tiles():
                sp.wait_ge(tiles_ready, 1)
                for par in range(2):
                    sp.wait_ge(scattered[par], 16 * TOP * G * ((ROUTED + 1 - par) // 2))
                load_tile(0, 0)
                load_tile(1, 1)

            phase1_steps(sp, step, first_tiles)
            for i in range(INTERLEAVED + 2, EARLY):
                load_tile(i, i % 2)
            sp.wait_ge(pad_at_ready, 1)
            for e in range(E):
                at = sp.value_load(pad_at[0:1, e:e + 1], min_val=0, max_val=E * REGION - TILE)
                sp.dma_start(routed[bass.ds(at, TILE), :].rearrange("(c p) w -> p c w", p=P),
                             pad_rows[:, :, :]).then_inc(pads_stored, 16)
            sp.wait_ge(pads_stored, 16 * E)
            sp.wait_ge(blank_stored, 16)
            for par in range(2):
                sp.wait_ge(scattered[par], 16 * TOP * G * NG // 2)
            sp.wait_ge(tiles_ready, 2)
            with sp.Fori(0, (NT - EARLY) // 2) as i:
                for k in range(2):
                    load_tile(i * 2 + (EARLY + k), (EARLY + k) % 2)

        @block.gpsimd
        def _(pool):
            steps = Steps(pool, pool_step)
            nc.gpsimd.memset(ident32[:, :], 0.0)
            nc.gpsimd.memset(ident16[:, :], 0.0)
            nc.gpsimd.memset(before[:, :], 1.0)
            nc.gpsimd.memset(ones[:, :], 1.0)
            nc.gpsimd.memset(up_to[:, :, :], 1.0)
            nc.gpsimd.memset(running[:, 0, :], 0.0)
            nc.gpsimd.memset(rows[:, :, :, D:ROW], 0.0)
            steps.link(nc.gpsimd.memset(pad_rows[:, :, :], 0.0))
            for ident in (ident32, ident16):
                nc.gpsimd.affine_select(out=ident[:, :], in_=ident[:, :], compare_op=ALU.not_equal, fill=1.0,
                                        base=0, pattern=[[-1, P]], channel_multiplier=1)
            nc.gpsimd.affine_select(out=before[:, :], in_=before[:, :], compare_op=ALU.is_gt, fill=0.0,
                                    base=0, pattern=[[1, P]], channel_multiplier=-1)
            nc.gpsimd.affine_select(out=up_to[:, :, :], in_=up_to[:, :, :], compare_op=ALU.is_ge, fill=0.0,
                                    base=0, pattern=[[1, E], [-1, E]], channel_multiplier=0)
            nc.gpsimd.iota(expert_no[:, :], pattern=[[1, E]], base=0, channel_multiplier=0,
                           allow_small_or_imprecise_dtypes=True)
            nc.gpsimd.iota(region_of[:, :], pattern=[[REGION, E]], base=0, channel_multiplier=0,
                           allow_small_or_imprecise_dtypes=True)
            nc.gpsimd.iota(tile_no[:, :], pattern=[[1, NTP]], base=0, channel_multiplier=0,
                           allow_small_or_imprecise_dtypes=True)
            nc.gpsimd.iota(token[:, :], pattern=[[P, G]], base=0, channel_multiplier=1)
            nc.gpsimd.iota(pad_rows[:, :, TOKEN].bitcast(I32), pattern=[[P, 2]], base=T,
                           channel_multiplier=1).then_inc(consts_ready, 1)
            pool.wait_ge(consts_ready, 1)
            pool.dma_start(routed[E * REGION:E * REGION + TILE, :].rearrange("(c p) w -> p c w", p=P),
                           pad_rows[:, :, :]).then_inc(blank_stored, 16)
            pool.dma_start(out[T:T + TILE, :].rearrange("(c p) d -> p c d", p=P),
                           pad_rows[:, :, 0:D]).then_inc(dump_stored, 16)

            def low_parts(n, par):
                for t in range(G):
                    pool.wait_ge(high_ready, n * G + t + 1)
                    nc.gpsimd.tensor_tensor(rows16[:, par, t, D:2 * D], xn2[:, par, t, :], rows16[:, par, t, 0:D],
                                            ALU.subtract).then_inc(low_ready, 1)

            def scatter(n, par):
                pool.wait_ge(low_ready, (n + 1) * G)
                pool.wait_ge(places_ready, n + 1)
                pool.sem_inc(pool_passed)
                for t in range(G):
                    for k in range(TOP):
                        pool.indirect_dma_start(
                            routed, bass.IndirectOffsetOnAxis(ap=slot_index[:, par, k, t:t + 1], axis=0),
                            rows[:, par, t, :], None).then_inc(scattered[par], 16)

            def add(i, par):
                pool.wait_ge(y_ready, i + 1)
                if not is_first(i):
                    pool.wait_ge(y_added, i * 32)
                pool.sem_inc(pool_passed)
                for c in range(2):
                    pool.indirect_dma_start(
                        out, bass.IndirectOffsetOnAxis(ap=target[:, par, c:c + 1], axis=0),
                        y[:, par, c, :], None, compute_op=ALU.add).then_inc(y_added, 16)

            def step(n, par, kind):
                if kind == "tiles":
                    low_parts(n - 1, 1 - par)
                    if is_first(n, LEAD + 2):
                        scatter(n - 2, par)
                    else:
                        i, tile_par = early(n, par, 0)
                        add(i - 1, 1 - tile_par)
                    add(*early(n, par, 0))
                    scatter(n - 1, 1 - par)
                    add(*early(n, par, 1))
                    return
                if kind == "last":
                    low_parts(n - 1, 1 - par)
                    scatter(n - 1, 1 - par)
                    return
                if kind == "end":
                    low_parts(n - 1, 1 - par)
                    add(INTERLEAVED - 1, (INTERLEAVED - 1) % 2)
                    scatter(n - 1, 1 - par)
                    return
                if not is_first(n):
                    low_parts(n - 1, 1 - par)
                if not is_first(n, 2):
                    scatter(n - 2, par)

            def stored(groups):
                pool.wait_ge(dump_stored, 16)
                for par in range(2):
                    pool.wait_ge(h1_stored[par], 16 * groups // 2)

            phase1_steps(pool, step, lambda: stored(LEAD))
            tiles_after(pool, add, lambda: None, lambda: stored(NG))
            pool.wait_ge(y_added, NT * 32)

        @block.scalar
        def _(act):
            act.wait_ge(degree_sum, 1)
            nc.scalar.activation(degree[:, 2:3], degree[:, 1:2], ACT.Sqrt).then_inc(degree_root, 1)

            def root(n, which, ready, done):
                act.wait_ge(ready, n + 1)
                nc.scalar.activation(std[:, which, :], mean_var[:, which, :, 1], ACT.Sqrt).then_inc(done, 1)

            def normalise1(n, par):
                act.wait_ge(norm1_ready, n + 1)
                for t in range(G):
                    nc.scalar.activation(xn[:, par, t, :], xg[:, par, t, :], ACT.Identity,
                                         bias=shift[:, 0, t:t + 1], scale=inv_std[:, 0, t:t + 1]
                                         ).then_inc(xn_ready, 1)

            def turn_x(i, par):
                act.wait_ge(x_turned, i + 1)
                nc.scalar.copy(xt[:, par, :, :, :].rearrange("p a c s -> p (a c s)"),
                               bank[TURN][:, :].bitcast(F16)).then_inc(xt_ready, 1)

            def tile(i, par, turn_next=True):
                def high(hc):
                    act.wait_ge(hid_ready, i * HC + hc + 1)
                    nc.scalar.copy(hh[:, par, 0, hc, :], hid[:, hc, :]).then_inc(hid_high, 1)

                if not is_first(i, 2):
                    act.wait_ge(down_ready, i - 1)
                for hc in range(HC):
                    act.wait_ge(up_ready, i * HC + hc + 1)
                    if not (is_first(i) and hc < 2):
                        act.wait_ge(hid_ready, i * HC + hc - 1)
                    nc.scalar.activation(silu[:, hc % 2, :], bank[hc][:, 0:TILE], ACT.Silu,
                                         scale=silu_scale[:, 0:1]).then_inc(silu_ready, 1)
                    if hc >= 1:
                        high(hc - 1)
                high(HC - 1)
                if turn_next and not (isinstance(i, int) and i == NT - 1):
                    turn_x(i + 1, 1 - par)
                act.wait_ge(margin_ready, i + 1)
                nc.scalar.activation(tanh[:, par, :], margin[:, par, :], ACT.Tanh, scale=0.5).then_inc(tanh_ready, 1)

            def take_z(n, t):
                act.wait_ge(z_ready, n * G + t + 1)
                if not (is_first(n) and t < 2):
                    act.wait_ge(gnn_ready, n * G + t - 1)
                nc.scalar.copy(zt[:, t % 2, :], bank[t % 2][:, 0:D]).then_inc(zt_ready, 1)

            def take_xn2(n, t):
                act.wait_ge(turned2, n * G + t + 1)
                if not (is_first(n) and t < 2):
                    act.wait_ge(logits_ready, n * G + t - 1)
                nc.scalar.copy(xn2t[:, t % 2, :], bank[t % 2][:, 0:D]).then_inc(xn2t_ready, 1)

            def normalise2(n, par):
                act.wait_ge(norm2_ready, n + 1)
                if not is_first(n, 2):
                    act.wait_ge(low_ready, (n - 1) * G)
                for t in range(G):
                    nc.scalar.activation(xn2[:, par, t, :], h1[:, par, t, :], ACT.Identity,
                                         bias=shift[:, 1, t:t + 1], scale=inv_std[:, 1, t:t + 1]
                                         ).then_inc(xn2_ready, 1)

            def high_parts(n, par, tiles):
                if not is_first(n, 2):
                    act.wait_ge(scattered[par], (n - par) * (8 * TOP * G))
                for t in tiles:
                    act.wait_ge(xn2_ready, n * G + t + 1)
                    nc.scalar.copy(rows16[:, par, t, 0:D], xn2[:, par, t, :]).then_inc(high_ready, 1)

            def square_weights(n, pieces):
                act.wait_ge(w_loaded[n], 48 * PAIR)
                if n >= 1:
                    act.wait_ge(squares_summed, n)
                for k, j in pieces:
                    at = (n * PAIR + k + 1) * SLOT + j * PIECE
                    nc.scalar.activation(squares[:, k, j * PIECE:(j + 1) * PIECE], weights[:, at:at + PIECE],
                                         ACT.Square).then_inc(squares_act, 1)

            def cut_weights(n, pieces):
                for piece in pieces:
                    e, j = (n - FIRST_CUT) * PAIR + piece // 3, piece % 3
                    act.wait_ge(w_low, e * 3 + (j + 1))
                    nc.scalar.activation(halves[:, bass.ds(e * (2 * SLOT) + j * 2 * PIECE, PIECE)],
                                         weights[:, bass.ds((e + 1) * SLOT + j * PIECE, PIECE)],
                                         ACT.Identity, scale=w_scale[:, 0:1]).then_inc(w_high, 1)

            root(0, 0, stats1_ready, std1_ready)
            act.wait_ge(x_loaded[0], 16)
            normalise1(0, 0)

            def lead_step(n, par, kind):
                def cut(*pieces):
                    if kind == "cut":
                        cut_weights(n, pieces)

                def square(*pieces):
                    if kind == "squares":
                        square_weights(n, pieces)

                take_z(n, 0)
                take_z(n, 1)
                root(n + 1, 0, stats1_ready, std1_ready)
                if not is_first(n):
                    high_parts(n - 1, 1 - par, range(0, 2))
                take_z(n, 2)
                cut(0)
                take_z(n, 3)
                if not is_first(n):
                    high_parts(n - 1, 1 - par, range(2, G))
                cut(1)
                square((0, 0))
                normalise1(n + 1, 1 - par)
                if not is_first(n):
                    take_xn2(n - 1, 0)
                    take_xn2(n - 1, 1)
                root(n, 1, stats2_ready, std2_ready)
                square((0, 1))
                if not is_first(n):
                    take_xn2(n - 1, 2)
                    take_xn2(n - 1, 3)
                cut(2, 3)
                normalise2(n, par)
                square((1, 0), (1, 1))
                if kind == "scales":
                    act.wait_ge(norm_ready, 1)
                    nc.scalar.activation(norm[:, 2:3], norm[:, 1:2], ACT.Sqrt).then_inc(root_ready, 1)
                cut(4, 5)

            def step(n, par, kind):
                more = not (isinstance(n, int) and n >= NG - 1)
                if kind == "last":
                    for t in range(G):
                        take_xn2(n - 1, t)
                    for t in range(G):
                        take_z(n, t)
                    root(n, 1, stats2_ready, std2_ready)
                    normalise2(n, par)
                    high_parts(n, par, range(G))
                    return
                if kind == "end":
                    take_xn2(n - 1, 0)
                    take_xn2(n - 1, 1)
                    turn_x(INTERLEAVED, INTERLEAVED % 2)
                    take_xn2(n - 1, 2)
                    take_xn2(n - 1, 3)
                    return
                if kind != "tiles":
                    lead_step(n, par, kind)
                    return
                for t in range(G):
                    take_z(n, t)
                if kind == "tiles":
                    turn_x(*early(n, par, 0))
                if more:
                    root(n + 1, 0, stats1_ready, std1_ready)
                root(n, 1, stats2_ready, std2_ready)
                if kind == "tiles":
                    tile(*early(n, par, 0), False)
                if not is_first(n):
                    take_xn2(n - 1, 0)
                    take_xn2(n - 1, 1)
                    if kind == "tiles":
                        turn_x(*early(n, par, 1))
                    take_xn2(n - 1, 2)
                    take_xn2(n - 1, 3)
                if kind == "tiles":
                    normalise2(n, par)
                    tile(*early(n, par, 1))
                    if more:
                        normalise1(n + 1, 1 - par)
                    high_parts(n, par, range(G))
                    tile(*early(n, par, 2), False)

            phase1_steps(act, step, lambda: high_parts(LEAD, LEAD % 2, range(G)))
            tiles_after(act, tile, lambda: None)

        @block.vector
        def _(dve):
            steps = Steps(dve, dve_step)
            link, mark = steps.link, steps.mark

            dve.wait_ge(adj_loaded, 16)
            link(nc.vector.tensor_reduce(degree[:, 0:1], adj_sb[:, :], AX_X, ALU.add))
            nc.vector.tensor_scalar(degree[:, 1:2], degree[:, 0:1], 2.0 ** -126, None, ALU.max).then_inc(degree_sum, 1)
            mark(nc.vector.tensor_scalar(degree[:, 0:1], degree[:, 0:1], 0.0, None, ALU.is_gt))
            dve.wait_ge(degree_root, 1)
            link(nc.vector.reciprocal(degree[:, 3:4], degree[:, 2:3]))
            link(nc.vector.tensor_tensor(degree[:, 1:2], degree[:, 3:4], degree[:, 0:1], ALU.mult))
            nc.vector.tensor_scalar(adj_sb[:, :], adj_sb[:, :], degree[:, 1:2], None, ALU.mult
                                    ).then_inc(adj_half, 1)
            dve.wait_ge(gnn_loaded, 32)
            for j in range(2):
                link(nc.vector.tensor_copy(bias_cut[:, j, :], bias_row[:, j, :]))
                link(nc.vector.tensor_tensor(bias_row[:, j + 1, :], bias_row[:, j, :], bias_cut[:, j, :],
                                             ALU.subtract))
            nc.vector.tensor_copy(bias_cut[:, 2, :], bias_row[:, 2, :]).then_inc(bias_cut_ready, 1)
            dve.wait_ge(router_loaded, 32)
            nc.vector.tensor_scalar(wg_scaled[:, :, :], wg_sb[:, :, :], 1.0 / X_SCALE, None, ALU.mult)
            dve.wait_ge(adj_turned, 1)
            nc.vector.tensor_scalar(adj_t[:, :], bank[TURN][:, 0:P], degree[:, 1:2], None, ALU.mult
                                    ).then_inc(setup_ready, 1)

            def stats_of(src, which, ready):
                for t in range(G):
                    mark(nc.vector.bn_aggr(mean_var[:, which, t, :], stats[:, which, t, :]))
                steps.wait()
                nc.vector.tensor_scalar(mean_var[:, which, :, 1], mean_var[:, which, :, 1], EPS, None, ALU.add
                                        ).then_inc(ready, 1)

            def statistics1(n, par):
                dve.wait_ge(x_loaded[par], ((n - par) * 8) + 16)
                for t in range(G):
                    mark(nc.vector.bn_stats(stats[:, 0, t, :], xg[:, par, t, :]))
                steps.wait()
                dve.sem_inc(dve_passed)
                stats_of(xg, 0, stats1_ready)

            def inverse(n, which, std_ready, ready, scale):
                dve.wait_ge(std_ready, n + 1)
                link(nc.vector.reciprocal(inv_std[:, which, :], std[:, which, :]))
                if scale != 1.0:
                    link(nc.vector.tensor_scalar(inv_std[:, which, :], inv_std[:, which, :], scale, None, ALU.mult))
                nc.vector.scalar_tensor_tensor(shift[:, which, :], mean_var[:, which, :, 0], -1.0,
                                               inv_std[:, which, :], ALU.mult, ALU.mult).then_inc(ready, 1)

            def residual(n, par, tiles=range(G)):
                if not is_first(n, 2):
                    dve.wait_ge(h1_stored[par], (n - par) * 8)
                for t in tiles:
                    dve.wait_ge(gnn_ready, n * G + t + 1)
                    nc.vector.tensor_tensor(h1[:, par, t, :], bank[2 + t % 2][:, 0:D], xg[:, par, t, :], ALU.add
                                            ).then_inc(h1_done, 1)
                    if t >= 1:
                        dve.wait_ge(h1_done, n * G + t)
                        mark(nc.vector.bn_stats(stats[:, 1, t - 1, :], h1[:, par, t - 1, :]))
                if G - 1 not in tiles:
                    return
                dve.wait_ge(h1_done, n * G + G)
                mark(nc.vector.bn_stats(stats[:, 1, G - 1, :], h1[:, par, G - 1, :]))
                steps.wait()
                dve.sem_inc(dve_passed)
                stats_of(h1, 1, stats2_ready)

            def route(n, par):
                dve.wait_ge(logits_ready, (n + 1) * G)
                nc.vector.tensor_tensor(
                    logits[:, :, :], bank[ROUTER][:, 0:G * E].rearrange("p (t e) -> p t e", t=G),
                    bg_sb[:, :].unsqueeze(1).to_broadcast([P, G, E]), ALU.add).then_inc(logits_taken, 1)
                dve.wait_ge(logits_taken, n + 1)
                dve.sem_inc(dve_passed)
                for t in range(G):
                    mark(nc.vector.max(top8[:, t, :], logits[:, t, :]))
                steps.wait()
                dve.sem_inc(dve_passed)
                for t in range(G):
                    mark(nc.vector.max_index(top_index[:, t, :], top8[:, t, :], logits[:, t, :]))
                steps.wait()
                for k in range(TOP):
                    mark(nc.vector.tensor_tensor(onehot[:, k, :, :],
                                                 expert_no[:, :].unsqueeze(1).to_broadcast([P, G, E]),
                                                 top_index[:, :, k].unsqueeze(2).to_broadcast([P, G, E]),
                                                 ALU.is_equal))
                steps.wait()
                if not is_first(n, 2):
                    dve.wait_ge(scattered[par], (n - par) * (8 * TOP * G))
                nc.vector.tensor_tensor(picks[:, :, :], onehot[:, 0, :, :], onehot[:, 1, :, :], ALU.add
                                        ).then_inc(picks_ready, 1)
                nc.vector.tensor_tensor(rows[:, par, :, MARGIN], top8[:, :, 0], top8[:, :, 1], ALU.subtract)
                nc.vector.tensor_copy(rows[:, par, :, FIRST], top_index[:, :, 0])
                mark(nc.vector.tensor_copy(rows[:, par, :, TOKEN].bitcast(I32), token[:, :]))
                dve.wait_ge(picks_ready, n + 1)
                link(nc.vector.tensor_reduce(picks_sum[:, :], picks[:, :, :].rearrange("p t e -> p e t"),
                                             AX_X, ALU.add))
                mark(nc.vector.tensor_scalar(token[:, :], token[:, :], G * P, None, ALU.add))
                if not is_first(n):
                    dve.wait_ge(running_ready, n)
                nc.vector.tensor_tensor(running[:, 1 - par, :], running[:, par, :], picks_sum[:, :], ALU.add
                                        ).then_inc(running_ready, 1)

            def places(n, par):
                dve.wait_ge(before_ready, n + 1)
                link(nc.vector.tensor_tensor(place[:, :, :], bank[ROUTER][:, 0:G * E].rearrange("p (t e) -> p t e", t=G),
                                             region_of[:, :].unsqueeze(1).to_broadcast([P, G, E]), ALU.add))
                for k in range(TOP):
                    mark(nc.vector.tensor_tensor(place_of[:, k, :, :], onehot[:, k, :, :], place[:, :, :], ALU.mult))
                steps.wait()
                link(nc.vector.tensor_reduce(slot_of[:, :, :], place_of[:, :, :, :], AX_X, ALU.add))
                nc.vector.tensor_copy(slot_index[:, par, :, :], slot_of[:, :, :]).then_inc(places_ready, 1)


            def scales():
                one = Steps(dve, scale_step)
                dve.wait_ge(root_ready, 1)
                one.link(nc.vector.tensor_scalar(low2[:, :].bitcast(I32), norm[:, 2:3].bitcast(I32),
                                                 0x7F800000, None, ALU.bitwise_and))
                one.link(nc.vector.tensor_scalar(inv2[:, :].bitcast(I32), low2[:, :].bitcast(I32),
                                                 0x7F800000, None, ALU.bitwise_xor))
                nc.vector.tensor_scalar(w_scale[:, :], inv2[:, :], 2.0 ** 12, None, ALU.mult)
                nc.vector.tensor_scalar(silu_scale[:, :], low2[:, :], 2.0 ** -13 / X_SCALE, None, ALU.mult)
                nc.vector.tensor_scalar(up_scale[:, :], inv2[:, :], 2.0 ** -9 / X_SCALE, None, ALU.mult)
                one.link(nc.vector.tensor_tensor(cube2[:, :], low2[:, :], low2[:, :], ALU.mult))
                one.link(nc.vector.scalar_tensor_tensor(y_scale[:, :], cube2[:, :], 2.0 ** -19, low2[:, :],
                                                        ALU.mult, ALU.mult))
                dve.sem_inc(w_low, 3)

            def low_weights(n, pieces):
                for piece in pieces:
                    e, j = (n - FIRST_CUT) * PAIR + piece // 3, piece % 3
                    dve.wait_ge(w_high, e * 3 + (j + 1))
                    nc.vector.scalar_tensor_tensor(
                        halves[:, bass.ds(e * (2 * SLOT) + (2 * j + 1) * PIECE, PIECE)],
                        weights[:, bass.ds((e + 1) * SLOT + j * PIECE, PIECE)], w_scale[:, 0:1],
                        halves[:, bass.ds(e * (2 * SLOT) + 2 * j * PIECE, PIECE)], ALU.mult, ALU.subtract
                    ).then_inc(w_low, 1)

            table = Steps(dve, table_step)

            def shared_out(c0, c1, number, taken, start):
                n = c1 - c0
                table.link(nc.vector.tensor_tensor(upto[:, :, :], up_to[:, :, :],
                                                   number[:, :].unsqueeze(1).to_broadcast([P, E, E]), ALU.mult))
                table.link(nc.vector.tensor_reduce(ends[:, :], upto[:, :, :], AX_X, ALU.add))
                table.link(nc.vector.tensor_tensor(
                    past[:, 0:n, :], tile_no[:, 0:n].unsqueeze(2).to_broadcast([P, n, E]),
                    ends[:, :].unsqueeze(1).to_broadcast([P, n, E]), ALU.is_ge))
                table.mark(nc.vector.tensor_reduce(tile_expert[:, c0:c1], past[:, 0:n, :], AX_X, ALU.add))
                table.link(nc.vector.tensor_tensor(past_coef[:, 0:n, :], past[:, 0:n, :],
                                                   taken[:, :].unsqueeze(1).to_broadcast([P, n, E]), ALU.mult))
                table.link(nc.vector.tensor_reduce(tile_tmp[:, 0, 0:n], past_coef[:, 0:n, :], AX_X, ALU.add))
                table.mark(nc.vector.tensor_tensor(tile_tmp[:, 1, 0:n], tile_no[:, 0:n], tile_tmp[:, 0, 0:n],
                                                   ALU.subtract))
                table.link(nc.vector.tensor_scalar(tile_tmp[:, 2, 0:n], tile_expert[:, c0:c1], float(E),
                                                   float(TILE), ALU.is_lt, ALU.mult))
                table.link(nc.vector.scalar_tensor_tensor(tile_tmp[:, 3, 0:n], tile_tmp[:, 1, 0:n], start,
                                                          tile_tmp[:, 2, 0:n], ALU.add, ALU.mult))
                nc.vector.scalar_tensor_tensor(tile_row[:, c0:c1], tile_expert[:, c0:c1], float(REGION),
                                               tile_tmp[:, 3, 0:n], ALU.mult, ALU.add)
                nc.vector.tensor_scalar(tile_weights[:, c0:c1], tile_expert[:, c0:c1], float(E - 1),
                                        float(2 * SLOT), ALU.min, ALU.mult).then_inc(tiles_ready, 1)

            def counted(times, dst, rounding):
                dve.wait_ge(counts_ready, times)
                table.link(nc.vector.tensor_copy(count[:, :], bank[ROUTER if times == 2 else SUM][:, 0:E]))
                if times == 2:
                    table.link(nc.vector.tensor_tensor(expert_tmp[:, 0, :], count[:, :], region_of[:, :], ALU.add))
                    nc.vector.tensor_copy(pad_at[:, :], expert_tmp[:, 0, :]).then_inc(pad_at_ready, 1)
                table.link(nc.vector.tensor_scalar(count_i[:, 0, :], count[:, :], float(rounding), None, ALU.add))
                table.link(nc.vector.tensor_scalar(count_i[:, 1, :], count_i[:, 0, :], TILE.bit_length() - 1, None,
                                                   ALU.logical_shift_right))
                table.link(nc.vector.tensor_copy(dst[:, :], count_i[:, 1, :]))

            def early_table():
                counted(1, full, 0)
                shared_out(0, EARLY, full, full, 0.0)
                table.mark(nc.vector.memset(first[:, E:E + 1], 0.0))
                table.link(nc.vector.tensor_tensor(expert_tmp[:, 0, :], full[:, :], ends[:, :], ALU.subtract))
                table.link(nc.vector.tensor_scalar(expert_tmp[:, 1, :], expert_tmp[:, 0, :], float(EARLY), 0.0,
                                                   ALU.add, ALU.max))
                table.link(nc.vector.tensor_tensor(first[:, 0:E], expert_tmp[:, 1, :], full[:, :], ALU.min))

            def late_table():
                counted(2, whole, TILE - 1)
                table.mark(nc.vector.tensor_tensor(left[:, :], whole[:, :], first[:, 0:E], ALU.subtract))
                table.link(nc.vector.tensor_tensor(coef[:, :], whole[:, :], first[:, 1:E + 1], ALU.subtract))
                shared_out(EARLY, NT, left, coef, first[:, 0:1])

            def read_meta(i, par):
                dve.wait_ge(rows_loaded[par], (i - par) * 8 + 16)
                if not is_first(i, 2):
                    dve.wait_ge(y_added, (i - 1) * 32)
                nc.vector.tensor_copy(target[:, par, :], xr[:, par, :, TOKEN].bitcast(I32))
                nc.vector.tensor_scalar(own[:, par, :], xr[:, par, :, FIRST], tile_expert[:, bass.ds(i, 1)], 2.0,
                                        ALU.is_equal, ALU.mult).then_inc(own_ready, 1)
                dve.wait_ge(own_ready, i + 1)
                nc.vector.scalar_tensor_tensor(margin[:, par, :], own[:, par, :], 1.0, xr[:, par, :, MARGIN],
                                               ALU.subtract, ALU.mult).then_inc(margin_ready, 1)

            def tile(i, par, turn_next=True):
                def low(hc):
                    dve.wait_ge(hid_high, i * HC + hc + 1)
                    nc.vector.tensor_tensor(hh[:, par, 1, hc, :], hid[:, hc, :], hh[:, par, 0, hc, :],
                                            ALU.subtract).then_inc(hid_low, 1)

                for hc in range(HC):
                    dve.wait_ge(silu_ready, i * HC + hc + 1)
                    if not is_first(i):
                        dve.wait_ge(hid_low, (i - 1) * HC + hc + 1)
                    nc.vector.scalar_tensor_tensor(hid[:, hc, :], bank[hc][:, TILE:2 * TILE], up_scale[:, 0:1],
                                                   silu[:, hc % 2, :], ALU.mult, ALU.mult).then_inc(hid_ready, 1)
                    if hc >= 1:
                        low(hc - 1)
                low(HC - 1)
                read_meta(i, par)
                if not is_first(i):
                    scale_y(i - 1, 1 - par)
                dve.wait_ge(tanh_ready, i + 1)
                nc.vector.tensor_scalar(gate[:, par, :], tanh[:, par, :], 1.0, y_scale[:, 0:1], ALU.add, ALU.mult
                                        ).then_inc(gate_ready, 1)

            def scale_y(i, par):
                dve.wait_ge(gate_ready, i + 1)
                dve.wait_ge(down_ready, i + 1)
                for c in range(2):
                    last = nc.vector.tensor_scalar(y[:, par, c, :], bank[DOWN[par]][:, c * D:(c + 1) * D],
                                                   gate[:, par, c:c + 1], None, ALU.mult)
                last.then_inc(y_ready, 1)

            dve.wait_ge(consts_ready, 1)
            statistics1(0, 0)
            inverse(0, 0, std1_ready, norm1_ready, 1.0)

            def lead_step(n, par, kind):
                def low(*pieces):
                    if kind == "cut":
                        low_weights(n, pieces)

                def square(k):
                    if kind != "squares":
                        return
                    dve.wait_ge(w_loaded[n], 48 * PAIR)
                    if n >= 1:
                        dve.wait_ge(squares_summed, n)
                    piece = weights[:, (n * PAIR + k + 2) * SLOT - PIECE:(n * PAIR + k + 2) * SLOT]
                    nc.vector.tensor_tensor(squares[:, k, SLOT - PIECE:SLOT], piece, piece, ALU.mult
                                            ).then_inc(squares_dve, 1)

                statistics1(n + 1, 1 - par)
                if not is_first(n, 2):
                    route(n - 2, par)
                inverse(n + 1, 0, std1_ready, norm1_ready, 1.0)
                residual(n, par, range(0, 2))
                if not is_first(n, 2):
                    places(n - 2, par)
                low(0)
                square(0)
                residual(n, par, range(2, G))
                inverse(n, 1, std2_ready, norm2_ready, X_SCALE)
                square(1)
                low(1, 2, 3, 4, 5)
                if kind == "scales":
                    dve.wait_ge(squares_summed, SQUARES)
                    nc.vector.tensor_reduce(norm[:, 0:1], bank[SUM][:, :], AX_X, ALU.max).then_inc(sum_taken, 1)
                    dve.wait_ge(sum_taken, 1)
                    nc.vector.tensor_scalar(norm[:, 1:2], norm[:, 0:1], 1.05, 2.0 ** -60, ALU.mult, ALU.max
                                            ).then_inc(norm_ready, 1)
                    scales()

            def step(n, par, kind):
                if kind == "last":
                    route(n - 1, 1 - par)
                    residual(n, par, range(0, 2))
                    places(n - 1, 1 - par)
                    residual(n, par, range(2, G))
                    inverse(n, 1, std2_ready, norm2_ready, X_SCALE)
                    return
                if kind == "end":
                    route(n - 1, 1 - par)
                    return
                if kind != "tiles":
                    lead_step(n, par, kind)
                    return
                residual(n, par, range(0, 2))
                statistics1(n + 1, 1 - par)
                if is_first(n, LEAD + 2):
                    places(n - 2, par)
                residual(n, par, range(2, G))
                tile(*early(n, par, 0))
                inverse(n + 1, 0, std1_ready, norm1_ready, 1.0)
                inverse(n, 1, std2_ready, norm2_ready, X_SCALE)
                route(n - 1, 1 - par)
                tile(*early(n, par, 1))
                places(n - 1, 1 - par)
                tile(*early(n, par, 2))

            def table_and_route():
                early_table()
                route(LEAD - 1, (LEAD - 1) % 2)

            def places_and_table():
                places(NG - 1, (NG - 1) % 2)
                late_table()

            phase1_steps(dve, step, table_and_route, steps)
            tiles_after(dve, tile, places_and_table)
            scale_y(NT - 1, (NT - 1) % 2)

        @block.tensor
        def _(pe):
            pe.wait_ge(consts_ready, 1)
            pe.wait_ge(adj_half, 1)
            nc.tensor.transpose(bank[TURN][:, 0:P], adj_sb[:, :], ident32[:, :]).then_inc(adj_turned, 1)
            pe.wait_ge(setup_ready, 1)
            pe.wait_ge(bias_moved, 48)

            def z(n, par, t):
                pe.wait_ge(xn_ready, n * G + t + 1)
                for c in range(KC):
                    mm = nc.tensor.matmul(bank[t % 2][:, c * P:(c + 1) * P], xn[:, par, t, c * P:(c + 1) * P],
                                          adj_t[:, :], start=True, stop=True)
                mm.then_inc(z_ready, 1)

            def gnn(n, t):
                pe.wait_ge(zt_ready, n * G + t + 1)
                if not (is_first(n) and t < 2):
                    pe.wait_ge(h1_done, n * G + t - 1)
                o = bank[2 + t % 2][:, 0:D]
                nc.tensor.matmul(o, ones[0:3, :], bias3[:, :], start=True, stop=False)
                for c in range(KC):
                    mm = nc.tensor.matmul(o, zt[:, t % 2, c * P:(c + 1) * P], gw_sb[:, c, :],
                                          start=False, stop=(c == KC - 1))
                mm.then_inc(gnn_ready, 1)

            def turn2(n, par, t):
                pe.wait_ge(xn2_ready, n * G + t + 1)
                for c in range(KC):
                    mm = nc.tensor.transpose(bank[t % 2][:, c * P:(c + 1) * P],
                                             xn2[:, par, t, c * P:(c + 1) * P], ident32[:, :])
                mm.then_inc(turned2, 1)

            def router(n, t):
                pe.wait_ge(xn2t_ready, n * G + t + 1)
                if t == 0 and not is_first(n):
                    pe.wait_ge(places_ready, n)
                for c in range(KC):
                    mm = nc.tensor.matmul(bank[ROUTER][:, t * E:(t + 1) * E], xn2t[:, t % 2, c * P:(c + 1) * P],
                                          wg_scaled[:, c, :], start=(c == 0), stop=(c == KC - 1))
                mm.then_inc(logits_ready, 1)

            def picks_before(n, par):
                pe.wait_ge(picks_ready, n + 1)
                o = bank[ROUTER]
                nc.tensor.matmul(o[:, 0:G * E], before[:, :], picks[:, :, :].rearrange("p t e -> p (t e)"),
                                 start=True, stop=False)
                for t in range(G - 1):
                    nc.tensor.matmul(o[:, (t + 1) * E:G * E], ones[:, :],
                                     picks[:, t, :].unsqueeze(1).to_broadcast([P, G - 1 - t, E]),
                                     start=False, stop=False)
                nc.tensor.matmul(o[:, 0:G * E], ones[:, :], running[:, par, :].unsqueeze(1).to_broadcast([P, G, E]),
                                 start=False, stop=True).then_inc(before_ready, 1)

            def sum_squares(n):
                for k in range(PAIR):
                    pe.wait_ge(squares_act, (n * PAIR + k + 1) * 2)
                    pe.wait_ge(squares_dve, n * PAIR + k + 1)
                    for j in range(SLOT // 512):
                        mm = nc.tensor.matmul(bank[SUM][:, :], ones[:, :], squares[:, k, j * 512:(j + 1) * 512],
                                              start=(n == 0 and k == 0 and j == 0),
                                              stop=(n == SQUARES - 1 and k == PAIR - 1 and j == SLOT // 512 - 1))
                mm.then_inc(squares_summed, 1)

            def counts(groups, in_bank):
                pe.wait_ge(running_ready, groups)
                pe.wait_ge(places_ready, groups)
                nc.tensor.matmul(bank[in_bank][:, 0:E], ones[:, :], running[:, groups % 2, :], start=True, stop=True
                                 ).then_inc(counts_ready, 1)

            def turn_x(i, par):
                pe.wait_ge(rows_loaded[par], (i - par) * 8 + 16)
                if not is_first(i):
                    pe.wait_ge(xt_ready, i)
                o = bank[TURN][:, :].bitcast(F16)
                for c in range(2):
                    for part in range(2):
                        for k in range(KC):
                            at = (part * KC + k) * TILE + c * P
                            mm = nc.tensor.transpose(o[:, at:at + P],
                                                     xr16[:, par, c, part * D + k * P:part * D + (k + 1) * P],
                                                     ident16[:, :])
                mm.then_inc(x_turned, 1)

            def down(i, par):
                w = pe.value_load(tile_weights[0:1, bass.ds(i, 1)], min_val=0, max_val=(E - 1) * 2 * SLOT)
                pe.wait_ge(hid_low, (i + 1) * HC)
                if not is_first(i, 2):
                    pe.wait_ge(y_ready, i - 1)
                for c in range(2):
                    terms = [(hc, a, b) for hc in range(HC) for a, b in ((0, 0), (0, 1), (1, 0))]
                    for j, (hc, a, b) in enumerate(terms):
                        mm = nc.tensor.matmul(bank[DOWN[par]][:, c * D:(c + 1) * D],
                                              hh[:, par, a, hc, c * P:(c + 1) * P],
                                              halves[:, bass.ds(w + ((4 + b) * PIECE + hc * D), D)],
                                              start=(j == 0), stop=(j == len(terms) - 1))
                mm.then_inc(down_ready, 1)

            def tile(i, par, turn_next=True, h1_taken=None):
                w = pe.value_load(tile_weights[0:1, bass.ds(i, 1)], min_val=0, max_val=(E - 1) * 2 * SLOT)
                pe.wait_ge(xt_ready, i + 1)
                for hc in range(HC):
                    if not is_first(i):
                        pe.wait_ge(hid_ready, (i - 1) * HC + hc + 1)
                    if hc == 2 and h1_taken is not None:
                        pe.wait_ge(h1_done, h1_taken)
                    for side in range(2):
                        terms = [(k, a, b) for k in range(KC) for a, b in ((0, 0), (0, 1), (1, 0))]
                        for j, (k, a, b) in enumerate(terms):
                            mm = nc.tensor.matmul(
                                bank[hc][:, side * TILE:(side + 1) * TILE],
                                halves[:, bass.ds(w + ((2 * side + a) * PIECE + k * HID + hc * P), P)],
                                xt[:, par, b, k, :], start=(j == 0), stop=(j == len(terms) - 1))
                    mm.then_inc(up_ready, 1)
                if turn_next and not (isinstance(i, int) and i == NT - 1):
                    turn_x(i + 1, 1 - par)
                if not is_first(i):
                    down(i - 1, 1 - par)

            def finish(n, par, before_router=lambda: None):
                turn2(n, par, 0)
                turn2(n, par, 1)
                before_router()
                router(n, 0)
                for t in range(1, G):
                    if t + 1 < G:
                        turn2(n, par, t + 1)
                    router(n, t)

            def step(n, par, kind):
                if kind == "end":
                    finish(n - 1, 1 - par, lambda: turn_x(INTERLEAVED, INTERLEAVED % 2))
                    return
                if kind == "last":
                    finish(n - 1, 1 - par)
                if kind != "end":
                    z(n, par, 0)
                    for t in range(G):
                        if t + 1 < G:
                            z(n, par, t + 1)
                        if kind == "tiles" and t == 3:
                            turn_x(*early(n, par, 0))
                        gnn(n, t)
                        if t == 1 and kind == "last":
                            picks_before(n - 1, 1 - par)
                        elif t == 1 and (kind != "tiles" or is_first(n, LEAD + 2)) and not is_first(n, 2):
                            picks_before(n - 2, par)
                if is_first(n, LEAD + 2) and kind == "tiles":
                    pe.wait_ge(tiles_ready, 1)
                    pe.wait_ge(w_low, 3 * E + 3)
                if kind == "tiles":
                    i, tile_par = early(n, par, 0)
                    tile(i, tile_par, False, (n + 1) * G)
                    pe.wait_ge(hid_ready, (i + 1) * HC)
                if kind in ("squares", "scales") and n >= 1:
                    sum_squares(n - 1)
                if kind == "tiles":
                    finish(n - 1, 1 - par, lambda: turn_x(*early(n, par, 1)))
                    tile(*early(n, par, 1))
                    picks_before(n - 1, 1 - par)
                elif kind != "last" and not is_first(n):
                    finish(n - 1, 1 - par)
                if kind == "tiles":
                    i, tile_par = early(n, par, 2)
                    tile(i, tile_par, False)
                    pe.wait_ge(hid_ready, (i + 1) * HC)

            def last_counts():
                picks_before(NG - 1, (NG - 1) % 2)
                counts(NG, ROUTER)

            phase1_steps(pe, step, lambda: counts(ROUTED, SUM))
            tiles_after(pe, tile, last_counts, lambda: pe.wait_ge(tiles_ready, 2))
            down(NT - 1, (NT - 1) % 2)


_INS = ["x", "adj", "L0_gnn_weight", "L0_gnn_bias", "L0_ffn_Wg", "L0_ffn_bg", "L0_ffn_W1", "L0_ffn_W3", "L0_ffn_W2"]
PAD_ROWS = 2 * P


def kernel(**inputs):
    import numpy as _np
    import concourse.bacc as _bacc
    from concourse import mybir as _mybir
    from concourse.bass_utils import run_bass_kernel_spmd as _run

    nc = _bacc.Bacc("TRN2", target_bir_lowering=False, num_devices=1)
    arrays, args = {}, []
    for name in _INS:
        a = _np.ascontiguousarray(inputs[name])
        arrays[f"in_{name}_dram"] = a
        args.append(nc.dram_tensor(f"in_{name}_dram", a.shape, _mybir.dt.from_np(a.dtype), kind="ExternalInput").ap())
    b, n, d = inputs["x"].shape
    out = nc.dram_tensor("out_0_dram", (b * n + PAD_ROWS, d), F32, kind="ExternalOutput").ap()
    build(nc, *args, out)
    r = _run(nc, [arrays], core_ids=[0])
    return r.results[0]["out_0_dram"][:b * n].reshape(b, n, d)
```

```python
from contextlib import ExitStack

import concourse.bass as bass
from concourse import mybir

ALU = mybir.AluOpType
ACT = mybir.ActivationFunctionType
F32 = mybir.dt.float32
F16 = mybir.dt.float16
BF16 = mybir.dt.bfloat16
I32 = mybir.dt.int32
U32 = mybir.dt.uint32
AX_X = mybir.AxisListType.X
MAX_OVER_PARTITIONS = bass.bass_isa.ReduceOp.max

P = 128
EPS = 1e-5


class Steps:

    def __init__(self, engine, semaphore):
        self.engine, self.semaphore, self.at, self.done = engine, semaphore, 0, 0

    def mark(self, instruction):
        instruction.then_inc(self.semaphore, 1)
        self.done += 1

    def wait(self):
        self.engine.wait_ge(self.semaphore, self.at + self.done)

    def link(self, instruction):
        self.mark(instruction)
        self.wait()

    def restart(self, at):
        self.at, self.done = at, 0


def build(nc, x, adj, gnn_w, gnn_b, wg, bg, w1, w3, w2, out):
    B, N, D = x.shape
    E, _, HID = w1.shape
    T = B * N
    TOP = 2
    assert N == P and D == 2 * P and HID == 4 * P and T % (4 * P) == 0
    KC = D // P
    HC = HID // P
    G = 4
    NG = T // (G * P)
    TILE = 2 * P
    NT = T * TOP // TILE + E - 1
    NTP = NT + 1
    REGION = T + TILE
    ROW = D + 8
    TOKEN, MARGIN, FIRST = D, D + 1, D + 2
    PIECE = KC * HID
    SLOT = 3 * PIECE
    PER_GROUP = G * P * TOP // TILE
    LEAD = 7
    ROUTED = LEAD - 1
    EARLY = ROUTED * PER_GROUP - (E - 1)
    PER_STEP = 2
    SQUARES, CUTS = 4, 4
    PAIR = 2
    FIRST_CUT = SQUARES
    assert HC * D == PIECE and PAIR * SQUARES == E and PAIR * CUTS == E and FIRST_CUT + CUTS == LEAD + 1
    INTERLEAVED = PER_STEP * (NG - 2 - LEAD)
    assert (NG - LEAD) % 2 == 1 and INTERLEAVED < EARLY and (NT - EARLY) % 2 == 0
    DVE_PIECES = 5
    LOW_MADE = {0: DVE_PIECES - 1, 1: DVE_PIECES, 3: DVE_PIECES + 1, 4: DVE_PIECES + 2, 5: DVE_PIECES + 3}
    X_SCALE = 2.0 ** 11
    DVE_LINKS = {"cut": 36, "tiles": 36}
    ROUTER = 4
    DOWN = (5, 7)
    TURN = 6
    SUM = 7

    tokens_in = x.rearrange("b n d -> (b n) d")
    routed = nc.dram_tensor("routed", (E * REGION + TILE, ROW), F32).ap()

    with ExitStack() as ctx:
        def sb(name, shape, dt):
            return ctx.enter_context(nc.sbuf_tensor(name, shape, dt))

        def sem(name):
            return ctx.enter_context(nc.semaphore(name))

        bank = [ctx.enter_context(nc.psum_tensor(f"bank{i}", [P, 512], F32)) for i in range(8)]

        ident32 = sb("ident32", [P, P], F32)
        ident16 = sb("ident16", [P, P], F16)
        before = sb("before", [P, P], BF16)
        ones = sb("ones", [P, P], BF16)
        up_to = sb("up_to", [P, E, E], F32)
        expert_no = sb("expert_no", [P, E], F32)
        region_of = sb("region_of", [P, E], F32)
        tile_no = sb("tile_no", [P, NTP], F32)
        adj_sb = sb("adj_sb", [P, P], F32)
        adj_t = sb("adj_t", [P, P], F32)
        degree = sb("degree", [P, 4], F32)
        gw_sb = sb("gw_sb", [P, KC, D], F32)
        bias_row = sb("bias_row", [1, 3, D], F32)
        bias_cut = sb("bias_cut", [1, 3, D], BF16)
        bias3 = sb("bias3", [3, D], BF16)
        wg_sb = sb("wg_sb", [P, KC, E], F32)
        wg_squares = sb("wg_squares", [P, KC, E], BF16)
        wg_scaled = sb("wg_scaled", [P, KC, E], F32)
        wg16 = sb("wg16", [P, 2, KC, E], F16)
        wg_norm = sb("wg_norm", [P, 4], F32)
        wg_low2 = sb("wg_low2", [P, 1], F32)
        wg_inv2 = sb("wg_inv2", [P, 1], F32)
        logit_scale = sb("logit_scale", [P, 1], F32)
        bg_sb = sb("bg_sb", [P, E], F32)
        weights = sb("weights", [P, (E + 1) * SLOT], F32)
        halves = weights[:, :].bitcast(F16)
        shared = sb("shared", [P, 3 * HC * TILE], F32)
        squares = shared[:, :].bitcast(BF16).rearrange("p (k w) -> p k w", k=PAIR)
        assert PAIR * SLOT == 6 * HC * TILE
        norm = sb("norm", [P, 4], F32)
        low2 = sb("low2", [P, 1], F32)
        inv2 = sb("inv2", [P, 1], F32)
        cube2 = sb("cube2", [P, 1], F32)
        w_scale = sb("w_scale", [P, 1], F32)
        silu_scale = sb("silu_scale", [P, 1], F32)
        up_scale = sb("up_scale", [P, 1], F32)
        y_scale = sb("y_scale", [P, 1], F32)
        xg = sb("xg", [P, 2, G, D], F32)
        xn = sb("xn", [P, 2, G, D], F32)
        zt = sb("zt", [P, 2, D], F32)
        h1 = sb("h1", [P, 2, G, D], F32)
        xn2 = sb("xn2", [P, 2, G, D], F32)
        rows_t = sb("rows_t", [P, 2, 2, 2, KC, P], F16)
        rows = sb("rows", [P, 2, G, ROW], F32)
        rows16 = rows[:, :, :, :].bitcast(F16)
        stats = sb("stats", [P, 2, G, 6], F32)
        mean_var = sb("mean_var", [P, 2, G, 2], F32)
        std = sb("std", [P, 2, G], F32)
        inv_std = sb("inv_std", [P, 2, G], F32)
        shift = sb("shift", [P, 2, G], F32)
        logits = sb("logits", [P, G, E], F32)
        top8 = sb("top8", [P, G, 8], F32)
        top_index = sb("top_index", [P, G, 8], U32)
        onehot = sb("onehot", [P, TOP, G, E], F32)
        picks = sb("picks", [P, G, E], BF16)
        picks_sum = sb("picks_sum", [P, E], F32)
        running = sb("running", [P, 2, E], BF16)
        token = sb("token", [P, G], I32)
        place = sb("place", [P, G, E], F32)
        place_of = sb("place_of", [P, TOP, G, E], F32)
        slot_of = sb("slot_of", [P, TOP, G], F32)
        slot_index = sb("slot_index", [P, 2, TOP, G], U32)
        pad_rows = sb("pad_rows", [P, 2, ROW], F32)
        count = sb("count", [P, E], F32)
        count_i = sb("count_i", [P, 2, E], I32)
        full = sb("full", [P, E], F32)
        first = sb("first", [P, E + 1], F32)
        whole = sb("whole", [P, E], F32)
        left = sb("left", [P, E], F32)
        coef = sb("coef", [P, E], F32)
        upto = sb("upto", [P, E, E], F32)
        ends = sb("ends", [P, E], F32)
        past = sb("past", [P, NTP, E], F32)
        past_coef = sb("past_coef", [P, NTP, E], F32)
        tile_expert = sb("tile_expert", [P, NTP], F32)
        tile_tmp = sb("tile_tmp", [P, 4, NTP], F32)
        expert_tmp = sb("expert_tmp", [P, 2, E], F32)
        tile_row = sb("tile_row", [P, NTP], I32)
        tile_weights = sb("tile_weights", [P, NTP], I32)
        pad_at = sb("pad_at", [P, E], I32)
        xr = sb("xr", [P, 2, 2, ROW], F32)
        xr16 = xr[:, :, :, :].bitcast(F16)
        xt = sb("xt", [P, 2, 2, KC, TILE], F16)
        silu_of_one = sb("silu_of_one", [P, 1], F32)
        silu = sb("silu", [P, 2, TILE], F32)
        hid = shared[:, 0:HC * TILE].rearrange("p (c s) -> p c s", c=HC)
        hh = shared[:, HC * TILE:].bitcast(F16).rearrange("p (i a c s) -> p i a c s", i=2, a=2, c=HC)
        y = sb("y", [P, 2, 2, D], F32)
        target = sb("target", [P, 2, 2], U32)
        own = sb("own", [P, 2, 2], F32)
        margin = sb("margin", [P, 2, 2], F32)
        tanh = sb("tanh", [P, 2, 2], F32)
        gate = sb("gate", [P, 2, 2], F32)

        adj_loaded = sem("adj_loaded")
        bias_loaded = sem("bias_loaded")
        gnn_loaded = sem("gnn_loaded")
        router_loaded = sem("router_loaded")
        bias_moved = sem("bias_moved")
        x_loaded = [sem(f"x_loaded{i}") for i in range(2)]
        w_loaded = [sem(f"w_loaded{i}") for i in range(SQUARES)]
        h1_stored = [sem(f"h1_stored{i}") for i in range(2)]
        dump_stored = sem("dump_stored")
        blank_stored = sem("blank_stored")
        pads_stored = sem("pads_stored")
        scattered = [sem(f"scattered{i}") for i in range(2)]
        rows_loaded = [sem(f"rows_loaded{i}") for i in range(2)]
        y_added = sem("y_added")
        pool_passed = sem("pool_passed")
        dve_passed = sem("dve_passed")
        pool_step = sem("pool_step")
        dve_step = sem("dve_step")
        consts_ready = sem("consts_ready")
        degree_sum = sem("degree_sum")
        degree_root = sem("degree_root")
        adj_half = sem("adj_half")
        adj_turned = sem("adj_turned")
        bias_cut_ready = sem("bias_cut_ready")
        wg_squared = sem("wg_squared")
        wg_summed = sem("wg_summed")
        wg_max_taken = sem("wg_max_taken")
        wg_norm_ready = sem("wg_norm_ready")
        wg_root_ready = sem("wg_root_ready")
        wg_step = sem("wg_step")
        wg_ready = sem("wg_ready")
        setup_ready = sem("setup_ready")
        stats1_ready = sem("stats1_ready")
        std1_ready = sem("std1_ready")
        norm1_ready = sem("norm1_ready")
        xn_ready = sem("xn_ready")
        z_ready = sem("z_ready")
        zt_ready = sem("zt_ready")
        gnn_ready = sem("gnn_ready")
        h1_done = sem("h1_done")
        stats2_ready = sem("stats2_ready")
        std2_ready = sem("std2_ready")
        norm2_ready = sem("norm2_ready")
        xn2_ready = sem("xn2_ready")
        high_ready = sem("high_ready")
        low_ready = sem("low_ready")
        rows_turned = sem("rows_turned")
        rows_taken = [sem(f"rows_taken{i}") for i in range(2)]
        logits_ready = sem("logits_ready")
        logits_taken = sem("logits_taken")
        picks_ready = sem("picks_ready")
        before_ready = sem("before_ready")
        places_ready = sem("places_ready")
        squares_act = sem("squares_act")
        squares_dve = sem("squares_dve")
        squares_summed = sem("squares_summed")
        norm_ready = sem("norm_ready")
        root_ready = sem("root_ready")
        running_ready = sem("running_ready")
        silu_loaded = sem("silu_loaded")
        scales_ready = sem("scales_ready")
        w_high = sem("w_high")
        w_low = sem("w_low")
        w_low_pool = sem("w_low_pool")
        w_scaled_pool = sem("w_scaled_pool")
        counts_ready = sem("counts_ready")
        pad_at_ready = sem("pad_at_ready")
        tiles_ready = sem("tiles_ready")
        x_turned = sem("x_turned")
        xt_ready = sem("xt_ready")
        own_ready = sem("own_ready")
        gate_ready = sem("gate_ready")
        scale_step = sem("scale_step")
        table_step = sem("table_step")
        sum_taken = sem("sum_taken")
        margin_ready = sem("margin_ready")
        tanh_ready = sem("tanh_ready")
        up_ready = sem("up_ready")
        silu_ready = sem("silu_ready")
        hid_ready = sem("hid_ready")
        hid_high = sem("hid_high")
        hid_low = sem("hid_low")
        down_ready = sem("down_ready")
        y_ready = sem("y_ready")

        def phase1_steps(engine, step, between, steps=None):
            def pairs(n0, n1, kind):
                base = steps.at + steps.done if steps is not None else 0
                with engine.Fori(0, (n1 - n0) // 2) as i:
                    for k in range(2):
                        if steps is not None:
                            steps.restart(i * (2 * DVE_LINKS[kind]) + (base + k * DVE_LINKS[kind]))
                        step(i * 2 + (n0 + k), (n0 + k) % 2, kind)
                        assert steps is None or steps.done == DVE_LINKS[kind], (kind, steps.done)
                if steps is not None:
                    steps.restart(base + (n1 - n0) * DVE_LINKS[kind])

            for n in range(SQUARES):
                step(n, n % 2, "squares")
            step(SQUARES, SQUARES % 2, "scales")
            pairs(FIRST_CUT + 1, LEAD, "cut")
            step(LEAD, LEAD % 2, "cut")
            between()
            step(LEAD + 1, (LEAD + 1) % 2, "tiles")
            step(LEAD + 2, (LEAD + 2) % 2, "tiles")
            pairs(LEAD + 3, NG - 2, "tiles")
            step(NG - 2, (NG - 2) % 2, "tiles")
            step(NG - 1, (NG - 1) % 2, "last")
            step(NG, NG % 2, "end")

        def early(n, par, k):
            return (n - (LEAD + 1)) * PER_STEP + k, ((par - (LEAD + 1)) * PER_STEP + k) % 2

        def tiles_after(engine, tile, after={}):
            for i in range(INTERLEAVED, EARLY):
                tile(i, i % 2)
                if i in after:
                    after[i]()
            with engine.Fori(0, (NT - EARLY) // 2 - 1) as i:
                for k in range(2):
                    tile(i * 2 + (EARLY + k), (EARLY + k) % 2)
            tile(NT - 2, (NT - 2) % 2)
            tile(NT - 1, (NT - 1) % 2)

        def is_first(n, k=1):
            return isinstance(n, int) and n < k

        block = ctx.enter_context(nc.Block())

        @block.sync
        def _(sp):
            sp.dma_start(adj_sb[:, :], adj).then_inc(adj_loaded, 16)
            sp.dma_start(bias_row[:, 0, :], gnn_b.rearrange("(a d) -> a d", a=1)).then_inc(bias_loaded, 16)
            sp.dma_start(xg[:, 0, :, :], tokens_in[0:G * P, :].rearrange("(t p) d -> p t d", p=P)
                         ).then_inc(x_loaded[0], 16)
            sp.dma_start(gw_sb[:, :, :], gnn_w.rearrange("(c p) d -> p c d", p=P)).then_inc(gnn_loaded, 16)
            sp.dma_start(wg_sb[:, :, :], wg.rearrange("(c p) e -> p c e", p=P)).then_inc(router_loaded, 16)
            sp.dma_start(bg_sb[:, :], bg.partition_broadcast(P)).then_inc(router_loaded, 16)
            sp.dma_start(xg[:, 1, :, :], tokens_in[G * P:2 * G * P, :].rearrange("(t p) d -> p t d", p=P)
                         ).then_inc(x_loaded[1], 16)
            def load_weights(n):
                for e in range(n * PAIR, (n + 1) * PAIR):
                    for j, (w, c) in enumerate(((w1, KC), (w3, KC), (w2, HC))):
                        at = (e + 1) * SLOT + j * PIECE
                        sp.dma_start(weights[:, at:at + PIECE].rearrange("p (c h) -> p c h", c=c),
                                     w[e].rearrange("(c p) h -> p c h", p=P)).then_inc(w_loaded[n], 16)

            sp.wait_ge(bias_cut_ready, 1)
            for j in range(3):
                sp.dma_start(bias3[j:j + 1, :], bias_cut[:, j, :]).then_inc(bias_moved, 16)
            load_weights(0)

            def load_tile(i, par):
                if not is_first(i, 2):
                    sp.wait_ge(x_turned, i - 1)
                    sp.wait_ge(margin_ready, i - 1)
                at = sp.value_load(tile_row[0:1, bass.ds(i, 1)], min_val=0, max_val=E * REGION)
                sp.dma_start(xr[:, par, :, :],
                             routed[bass.ds(at, TILE), :].rearrange("(c p) w -> p c w", p=P)
                             ).then_inc(rows_loaded[par], 16)

            def step(n, par, kind):
                if kind != "end":
                    sp.wait_ge(h1_done, (n + 1) * G)
                    sp.dma_start(out[bass.ds(n * (G * P), G * P), :].rearrange("(t p) d -> p t d", p=P),
                                 h1[:, par, :, :]).then_inc(h1_stored[par], 16)
                    if not (isinstance(n, int) and n + 2 >= NG):
                        sp.dma_start(xg[:, par, :, :], tokens_in[bass.ds((n + 2) * (G * P), G * P), :].rearrange(
                            "(t p) d -> p t d", p=P)).then_inc(x_loaded[par], 16)
                if kind == "squares" and n + 1 < SQUARES:
                    load_weights(n + 1)
                if kind == "tiles":
                    for k in range(PER_STEP):
                        i, tile_par = early(n, par, k)
                        load_tile(i + 2, tile_par)

            def first_tiles():
                sp.wait_ge(tiles_ready, 1)
                for par in range(2):
                    sp.wait_ge(scattered[par], 16 * TOP * G * ((ROUTED + 1 - par) // 2))
                load_tile(0, 0)
                load_tile(1, 1)

            phase1_steps(sp, step, first_tiles)
            for i in range(INTERLEAVED + 2, EARLY):
                load_tile(i, i % 2)
            sp.wait_ge(pad_at_ready, 1)
            for e in range(E):
                at = sp.value_load(pad_at[0:1, e:e + 1], min_val=0, max_val=E * REGION - TILE)
                sp.dma_start(routed[bass.ds(at, TILE), :].rearrange("(c p) w -> p c w", p=P),
                             pad_rows[:, :, :]).then_inc(pads_stored, 16)
            sp.wait_ge(pads_stored, 16 * E)
            sp.wait_ge(blank_stored, 16)
            for par in range(2):
                sp.wait_ge(scattered[par], 16 * TOP * G * NG // 2)
            sp.wait_ge(tiles_ready, 2)
            with sp.Fori(0, (NT - EARLY) // 2) as i:
                for k in range(2):
                    load_tile(i * 2 + (EARLY + k), (EARLY + k) % 2)

        @block.gpsimd
        def _(pool):
            steps = Steps(pool, pool_step)
            nc.gpsimd.memset(ident32[:, :], 0.0)
            nc.gpsimd.memset(ident16[:, :], 0.0)
            nc.gpsimd.memset(before[:, :], 1.0)
            nc.gpsimd.memset(ones[:, :], 1.0)
            nc.gpsimd.memset(up_to[:, :, :], 1.0)
            nc.gpsimd.memset(running[:, 0, :], 0.0)
            nc.gpsimd.memset(rows[:, :, :, D:ROW], 0.0)
            steps.link(nc.gpsimd.memset(pad_rows[:, :, :], 0.0))
            for ident in (ident32, ident16):
                nc.gpsimd.affine_select(out=ident[:, :], in_=ident[:, :], compare_op=ALU.not_equal, fill=1.0,
                                        base=0, pattern=[[-1, P]], channel_multiplier=1)
            nc.gpsimd.affine_select(out=before[:, :], in_=before[:, :], compare_op=ALU.is_gt, fill=0.0,
                                    base=0, pattern=[[1, P]], channel_multiplier=-1)
            nc.gpsimd.affine_select(out=up_to[:, :, :], in_=up_to[:, :, :], compare_op=ALU.is_ge, fill=0.0,
                                    base=0, pattern=[[1, E], [-1, E]], channel_multiplier=0)
            nc.gpsimd.iota(expert_no[:, :], pattern=[[1, E]], base=0, channel_multiplier=0,
                           allow_small_or_imprecise_dtypes=True)
            nc.gpsimd.iota(region_of[:, :], pattern=[[REGION, E]], base=0, channel_multiplier=0,
                           allow_small_or_imprecise_dtypes=True)
            nc.gpsimd.iota(tile_no[:, :], pattern=[[1, NTP]], base=0, channel_multiplier=0,
                           allow_small_or_imprecise_dtypes=True)
            nc.gpsimd.iota(token[:, :], pattern=[[P, G]], base=0, channel_multiplier=1)
            nc.gpsimd.iota(pad_rows[:, :, TOKEN].bitcast(I32), pattern=[[P, 2]], base=T,
                           channel_multiplier=1).then_inc(consts_ready, 1)
            pool.wait_ge(consts_ready, 1)
            pool.dma_start(routed[E * REGION:E * REGION + TILE, :].rearrange("(c p) w -> p c w", p=P),
                           pad_rows[:, :, :]).then_inc(blank_stored, 16)
            pool.dma_start(out[T:T + TILE, :].rearrange("(c p) d -> p c d", p=P),
                           pad_rows[:, :, 0:D]).then_inc(dump_stored, 16)

            def low_parts(n, par):
                for t in range(G):
                    pool.wait_ge(high_ready, n * G + t + 1)
                    nc.gpsimd.tensor_tensor(rows16[:, par, t, D:2 * D], xn2[:, par, t, :], rows16[:, par, t, 0:D],
                                            ALU.subtract).then_inc(low_ready, 1)

            def scatter(n, par):
                pool.wait_ge(low_ready, (n + 1) * G)
                pool.wait_ge(places_ready, n + 1)
                pool.sem_inc(pool_passed)
                for t in range(G):
                    for k in range(TOP):
                        pool.indirect_dma_start(
                            routed, bass.IndirectOffsetOnAxis(ap=slot_index[:, par, k, t:t + 1], axis=0),
                            rows[:, par, t, :], None).then_inc(scattered[par], 16)

            def low_weights(n):
                e = (n - FIRST_CUT) * PAIR + 1
                piece = weights[:, bass.ds((e + 1) * SLOT + 2 * PIECE, PIECE)]
                pool.wait_ge(w_high, (n - FIRST_CUT + 1) * 3 * PAIR)
                pool.sem_inc(pool_passed)
                nc.gpsimd.tensor_tensor(piece, piece, w_scale[:, 0:1].to_broadcast([P, PIECE]), ALU.mult
                                        ).then_inc(w_scaled_pool, 1)
                pool.wait_ge(w_scaled_pool, n - FIRST_CUT + 1)
                pool.sem_inc(pool_passed)
                nc.gpsimd.tensor_tensor(halves[:, bass.ds(e * (2 * SLOT) + 5 * PIECE, PIECE)], piece,
                                        halves[:, bass.ds(e * (2 * SLOT) + 4 * PIECE, PIECE)], ALU.subtract
                                        ).then_inc(w_low_pool, 1)

            def add(i, par):
                pool.wait_ge(y_ready, i + 1)
                if not is_first(i):
                    pool.wait_ge(y_added, i * 32)
                pool.sem_inc(pool_passed)
                for c in range(2):
                    pool.indirect_dma_start(
                        out, bass.IndirectOffsetOnAxis(ap=target[:, par, c:c + 1], axis=0),
                        y[:, par, c, :], None, compute_op=ALU.add).then_inc(y_added, 16)

            def step(n, par, kind):
                if kind == "tiles":
                    low_parts(n - 1, 1 - par)
                    if is_first(n, LEAD + 2):
                        scatter(n - 2, par)
                    else:
                        i, tile_par = early(n, par, 0)
                        add(i - 1, 1 - tile_par)
                    scatter(n - 1, 1 - par)
                    add(*early(n, par, 0))
                    return
                if kind == "last":
                    low_parts(n - 1, 1 - par)
                    return
                if kind == "end":
                    low_parts(n - 1, 1 - par)
                    scatter(n - 2, par)
                    scatter(n - 1, 1 - par)
                    add(INTERLEAVED - 1, (INTERLEAVED - 1) % 2)
                    return
                if not is_first(n):
                    low_parts(n - 1, 1 - par)
                if not is_first(n, 2):
                    scatter(n - 2, par)
                if kind in ("scales", "cut"):
                    low_weights(n)

            def stored(groups):
                pool.wait_ge(dump_stored, 16)
                for par in range(2):
                    pool.wait_ge(h1_stored[par], 16 * groups // 2)

            phase1_steps(pool, step, lambda: stored(ROUTED))
            tiles_after(pool, add, {EARLY - 1: lambda: stored(NG)})
            pool.wait_ge(y_added, NT * 32)

        @block.scalar
        def _(act):
            act.wait_ge(degree_sum, 1)
            nc.scalar.activation(degree[:, 2:3], degree[:, 1:2], ACT.Sqrt).then_inc(degree_root, 1)

            def root(n, which, ready, done):
                act.wait_ge(ready, n + 1)
                nc.scalar.activation(std[:, which, :], mean_var[:, which, :, 1], ACT.Sqrt).then_inc(done, 1)

            def normalise1(n, par, tiles=range(G)):
                act.wait_ge(norm1_ready, n + 1)
                for t in tiles:
                    nc.scalar.activation(xn[:, par, t, :], xg[:, par, t, :], ACT.Identity,
                                         bias=shift[:, 0, t:t + 1], scale=inv_std[:, 0, t:t + 1]
                                         ).then_inc(xn_ready, 1)

            def turn_x(i, par):
                act.wait_ge(x_turned, i + 1)
                nc.scalar.copy(xt[:, par, :, :, :].rearrange("p a c s -> p (a c s)"),
                               bank[TURN][:, :].bitcast(F16)).then_inc(xt_ready, 1)

            def tile(i, par, turn_next=True, between=lambda hc: None):
                def high(hc):
                    act.wait_ge(hid_ready, i * HC + hc + 1)
                    nc.scalar.copy(hh[:, par, 0, hc, :], hid[:, hc, :]).then_inc(hid_high, 1)

                if not is_first(i, 2):
                    act.wait_ge(down_ready, i - 1)
                for hc in range(HC):
                    act.wait_ge(up_ready, i * HC + hc + 1)
                    if not (is_first(i) and hc < 2):
                        act.wait_ge(hid_ready, i * HC + hc - 1)
                    nc.scalar.activation(silu[:, hc % 2, :], bank[hc][:, 0:TILE], ACT.Silu,
                                         scale=silu_scale[:, 0:1]).then_inc(silu_ready, 1)
                    if hc >= 1:
                        high(hc - 1)
                    between(hc)
                high(HC - 1)
                if turn_next and not (isinstance(i, int) and i == NT - 1):
                    turn_x(i + 1, 1 - par)
                act.wait_ge(margin_ready, i + 1)
                nc.scalar.activation(tanh[:, par, :], margin[:, par, :], ACT.Tanh, scale=0.5).then_inc(tanh_ready, 1)

            def load_silu(times):
                if not is_first(times):
                    act.wait_ge(silu_loaded, times)
                nc.scalar.activation(silu_of_one[:, :], ones[:, 0:1], ACT.Silu).then_inc(silu_loaded, 1)

            def take_z(n, t):
                act.wait_ge(z_ready, n * G + t + 1)
                if not (is_first(n) and t < 2):
                    act.wait_ge(gnn_ready, n * G + t - 1)
                nc.scalar.copy(zt[:, t % 2, :], bank[t % 2][:, 0:D]).then_inc(zt_ready, 1)

            def take_rows(n, half):
                act.wait_ge(rows_turned, 2 * n + half + 1)
                if not is_first(n):
                    act.wait_ge(logits_ready, 2 * n)
                nc.scalar.copy(rows_t[:, half, :, :, :, :].rearrange("p t a c n -> p (t a c n)"),
                               bank[half][:, :].bitcast(F16)).then_inc(rows_taken[half], 1)

            def normalise2(n, par, tiles=range(G)):
                act.wait_ge(norm2_ready, n + 1)
                if not is_first(n, 2):
                    act.wait_ge(low_ready, (n - 1) * G)
                for t in tiles:
                    nc.scalar.activation(xn2[:, par, t, :], h1[:, par, t, :], ACT.Identity,
                                         bias=shift[:, 1, t:t + 1], scale=inv_std[:, 1, t:t + 1]
                                         ).then_inc(xn2_ready, 1)

            def high_parts(n, par, tiles=range(G)):
                if not is_first(n, 2):
                    act.wait_ge(scattered[par], (n - par) * (8 * TOP * G))
                for t in tiles:
                    act.wait_ge(xn2_ready, n * G + t + 1)
                    nc.scalar.copy(rows16[:, par, t, 0:D], xn2[:, par, t, :]).then_inc(high_ready, 1)

            def square_weights(n, pieces):
                if not pieces:
                    return
                act.wait_ge(w_loaded[n], 48 * PAIR)
                if n >= 1:
                    act.wait_ge(squares_summed, n)
                for k, j in pieces:
                    at = (n * PAIR + k + 1) * SLOT + j * PIECE
                    nc.scalar.activation(squares[:, k, j * PIECE:(j + 1) * PIECE], weights[:, at:at + PIECE],
                                         ACT.Square).then_inc(squares_act, 1)

            def cut_weights(n, pieces):
                for piece in pieces:
                    e, j = (n - FIRST_CUT) * PAIR + piece // 3, piece % 3
                    if piece != 2:
                        act.wait_ge(w_low, (n - FIRST_CUT) * DVE_PIECES + LOW_MADE[piece])
                    elif not is_first(n, FIRST_CUT + 1):
                        act.wait_ge(w_low_pool, n - FIRST_CUT)
                    nc.scalar.activation(halves[:, bass.ds(e * (2 * SLOT) + j * 2 * PIECE, PIECE)],
                                         weights[:, bass.ds((e + 1) * SLOT + j * PIECE, PIECE)],
                                         ACT.Identity, scale=w_scale[:, 0:1]).then_inc(w_high, 1)

            root(0, 0, stats1_ready, std1_ready)
            act.wait_ge(x_loaded[0], 16)
            normalise1(0, 0)

            def lead_step(n, par, kind):
                def cut(*pieces):
                    if kind in ("scales", "cut"):
                        cut_weights(n, pieces)

                def square(of, *pieces):
                    if kind == of and n >= 1:
                        square_weights(n - 1, pieces)

                take_z(n, 0)
                take_z(n, 1)
                root(n + 1, 0, stats1_ready, std1_ready)
                if not is_first(n):
                    high_parts(n - 1, 1 - par, range(0, 2))
                if kind == "cut":
                    cut(0)
                take_z(n, 2)
                if kind == "cut":
                    cut(1)
                square("scales", (0, 0))
                if not is_first(n):
                    high_parts(n - 1, 1 - par, range(2, G))
                take_z(n, 3)
                square("scales", (0, 1), (1, 0), (1, 1))
                square("squares", (0, 0))
                normalise1(n + 1, 1 - par)
                if not is_first(n):
                    take_rows(n - 1, 0)
                root(n, 1, stats2_ready, std2_ready)
                if is_first(n):
                    act.wait_ge(wg_norm_ready, 1)
                    nc.scalar.activation(wg_norm[:, 2:3], wg_norm[:, 1:2], ACT.Sqrt).then_inc(wg_root_ready, 1)
                if kind == "scales":
                    act.wait_ge(norm_ready, 1)
                    nc.scalar.activation(norm[:, 2:3], norm[:, 1:2], ACT.Sqrt).then_inc(root_ready, 1)
                square("squares", (0, 1))
                if kind == "scales":
                    cut(0, 1)
                cut(2, 3)
                normalise2(n, par)
                square("squares", (1, 0), (1, 1))
                cut(4, 5)

            def step(n, par, kind):
                if kind == "last":
                    take_z(n, 0)
                    take_z(n, 1)
                    root(n - 1, 1, stats2_ready, std2_ready)
                    take_z(n, 2)
                    take_z(n, 3)
                    for t in range(G):
                        normalise2(n - 1, 1 - par, [t])
                        high_parts(n - 1, 1 - par, [t])
                    take_rows(n - 1, 0)
                    root(n, 1, stats2_ready, std2_ready)
                    for t in range(G):
                        normalise2(n, par, [t])
                        high_parts(n, par, [t])
                elif kind == "end":
                    take_rows(n - 1, 0)
                    turn_x(INTERLEAVED, INTERLEAVED % 2)
                    load_silu(NG - 1 - (LEAD + 1))
                elif kind == "tiles":
                    def fill(hc):
                        if hc == 0:
                            high_parts(n - 1, 1 - par, range(2))
                        elif hc < HC - 1:
                            if not is_first(n, LEAD + 2):
                                normalise2(n - 1, 1 - par, [hc + 1])
                            high_parts(n - 1, 1 - par, [hc + 1])

                    take_z(n, 0)
                    take_z(n, 1)
                    if not is_first(n, LEAD + 2):
                        root(n - 1, 1, stats2_ready, std2_ready)
                    take_z(n, 2)
                    take_z(n, 3)
                    turn_x(*early(n, par, 0))
                    if not is_first(n, LEAD + 2):
                        normalise2(n - 1, 1 - par, range(2))
                    root(n + 1, 0, stats1_ready, std1_ready)
                    load_silu(n - (LEAD + 1))
                    tile(*early(n, par, 0), False, fill)
                    take_rows(n - 1, 0)
                    turn_x(*early(n, par, 1))
                    tile(*early(n, par, 1), False, lambda hc: normalise1(n + 1, 1 - par, [hc]))
                else:
                    lead_step(n, par, kind)

            phase1_steps(act, step, lambda: None)
            tiles_after(act, tile)

        @block.vector
        def _(dve):
            steps = Steps(dve, dve_step)
            link, mark = steps.link, steps.mark

            dve.wait_ge(adj_loaded, 16)
            link(nc.vector.tensor_reduce(degree[:, 0:1], adj_sb[:, :], AX_X, ALU.add))
            nc.vector.tensor_scalar(degree[:, 1:2], degree[:, 0:1], 2.0 ** -126, None, ALU.max).then_inc(degree_sum, 1)
            mark(nc.vector.tensor_scalar(degree[:, 0:1], degree[:, 0:1], 0.0, None, ALU.is_gt))
            dve.wait_ge(degree_root, 1)
            link(nc.vector.reciprocal(degree[:, 3:4], degree[:, 2:3]))
            link(nc.vector.tensor_tensor(degree[:, 1:2], degree[:, 3:4], degree[:, 0:1], ALU.mult))
            nc.vector.tensor_scalar(adj_sb[:, :], adj_sb[:, :], degree[:, 1:2], None, ALU.mult
                                    ).then_inc(adj_half, 1)
            dve.wait_ge(bias_loaded, 16)
            for j in range(2):
                link(nc.vector.tensor_copy(bias_cut[:, j, :], bias_row[:, j, :]))
                link(nc.vector.tensor_tensor(bias_row[:, j + 1, :], bias_row[:, j, :], bias_cut[:, j, :],
                                             ALU.subtract))
            nc.vector.tensor_copy(bias_cut[:, 2, :], bias_row[:, 2, :]).then_inc(bias_cut_ready, 1)
            dve.wait_ge(router_loaded, 32)
            nc.vector.tensor_tensor(wg_squares[:, :, :], wg_sb[:, :, :], wg_sb[:, :, :], ALU.mult
                                    ).then_inc(wg_squared, 1)
            dve.wait_ge(adj_turned, 1)
            nc.vector.tensor_scalar(adj_t[:, :], bank[TURN][:, 0:P], degree[:, 1:2], None, ALU.mult
                                    ).then_inc(setup_ready, 1)

            def stats_of(src, which, ready):
                for t in range(G):
                    mark(nc.vector.bn_aggr(mean_var[:, which, t, :], stats[:, which, t, :]))
                steps.wait()
                nc.vector.tensor_scalar(mean_var[:, which, :, 1], mean_var[:, which, :, 1], EPS, None, ALU.add
                                        ).then_inc(ready, 1)

            def statistics1(n, par):
                dve.wait_ge(x_loaded[par], ((n - par) * 8) + 16)
                for t in range(G):
                    mark(nc.vector.bn_stats(stats[:, 0, t, :], xg[:, par, t, :]))
                steps.wait()
                dve.sem_inc(dve_passed)
                stats_of(xg, 0, stats1_ready)

            def inverse(n, which, std_ready, ready, scale):
                dve.wait_ge(std_ready, n + 1)
                link(nc.vector.reciprocal(inv_std[:, which, :], std[:, which, :]))
                if scale != 1.0:
                    link(nc.vector.tensor_scalar(inv_std[:, which, :], inv_std[:, which, :], scale, None, ALU.mult))
                nc.vector.scalar_tensor_tensor(shift[:, which, :], mean_var[:, which, :, 0], -1.0,
                                               inv_std[:, which, :], ALU.mult, ALU.mult).then_inc(ready, 1)

            def residual(n, par, tiles=range(G)):
                if not is_first(n, 2):
                    dve.wait_ge(h1_stored[par], (n - par) * 8)
                for t in tiles:
                    dve.wait_ge(gnn_ready, n * G + t + 1)
                    nc.vector.tensor_tensor(h1[:, par, t, :], bank[2 + t % 2][:, 0:D], xg[:, par, t, :], ALU.add
                                            ).then_inc(h1_done, 1)
                    if t >= 1:
                        dve.wait_ge(h1_done, n * G + t)
                        mark(nc.vector.bn_stats(stats[:, 1, t - 1, :], h1[:, par, t - 1, :]))
                if G - 1 not in tiles:
                    return
                dve.wait_ge(h1_done, n * G + G)
                mark(nc.vector.bn_stats(stats[:, 1, G - 1, :], h1[:, par, G - 1, :]))
                steps.wait()
                dve.sem_inc(dve_passed)
                stats_of(h1, 1, stats2_ready)

            def take_rows(n):
                dve.wait_ge(rows_turned, 2 * n + 2)
                if not is_first(n):
                    dve.wait_ge(logits_ready, 2 * n)
                nc.vector.tensor_copy(rows_t[:, 1, :, :, :, :].rearrange("p t a c n -> p (t a c n)"),
                                      bank[1][:, :].bitcast(F16)).then_inc(rows_taken[1], 1)

            def route(n, par):
                dve.wait_ge(logits_ready, 2 * (n + 1))
                nc.vector.scalar_tensor_tensor(
                    logits[:, :, :], bank[ROUTER][:, 0:G * E].rearrange("p (t e) -> p t e", t=G), logit_scale[:, 0:1],
                    bg_sb[:, :].unsqueeze(1).to_broadcast([P, G, E]), ALU.mult, ALU.add).then_inc(logits_taken, 1)
                dve.wait_ge(logits_taken, n + 1)
                dve.sem_inc(dve_passed)
                for t in range(G):
                    mark(nc.vector.max(top8[:, t, :], logits[:, t, :]))
                steps.wait()
                dve.sem_inc(dve_passed)
                for t in range(G):
                    mark(nc.vector.max_index(top_index[:, t, :], top8[:, t, :], logits[:, t, :]))
                steps.wait()
                for k in range(TOP):
                    mark(nc.vector.tensor_tensor(onehot[:, k, :, :],
                                                 expert_no[:, :].unsqueeze(1).to_broadcast([P, G, E]),
                                                 top_index[:, :, k].unsqueeze(2).to_broadcast([P, G, E]),
                                                 ALU.is_equal))
                steps.wait()
                if not is_first(n, 2):
                    dve.wait_ge(scattered[par], (n - par) * (8 * TOP * G))
                nc.vector.tensor_tensor(picks[:, :, :], onehot[:, 0, :, :], onehot[:, 1, :, :], ALU.add
                                        ).then_inc(picks_ready, 1)
                nc.vector.tensor_tensor(rows[:, par, :, MARGIN], top8[:, :, 0], top8[:, :, 1], ALU.subtract)
                nc.vector.tensor_copy(rows[:, par, :, FIRST], top_index[:, :, 0])
                mark(nc.vector.tensor_copy(rows[:, par, :, TOKEN].bitcast(I32), token[:, :]))
                dve.wait_ge(picks_ready, n + 1)
                link(nc.vector.tensor_reduce(picks_sum[:, :], picks[:, :, :].rearrange("p t e -> p e t"),
                                             AX_X, ALU.add))
                mark(nc.vector.tensor_scalar(token[:, :], token[:, :], G * P, None, ALU.add))
                if not is_first(n):
                    dve.wait_ge(running_ready, n)
                nc.vector.tensor_tensor(running[:, 1 - par, :], running[:, par, :], picks_sum[:, :], ALU.add
                                        ).then_inc(running_ready, 1)

            def places(n, par):
                dve.wait_ge(before_ready, n + 1)
                link(nc.vector.tensor_tensor(place[:, :, :], bank[ROUTER][:, 0:G * E].rearrange("p (t e) -> p t e", t=G),
                                             region_of[:, :].unsqueeze(1).to_broadcast([P, G, E]), ALU.add))
                for k in range(TOP):
                    mark(nc.vector.tensor_tensor(place_of[:, k, :, :], onehot[:, k, :, :], place[:, :, :], ALU.mult))
                steps.wait()
                link(nc.vector.tensor_reduce(slot_of[:, :, :], place_of[:, :, :, :], AX_X, ALU.add))
                nc.vector.tensor_copy(slot_index[:, par, :, :], slot_of[:, :, :]).then_inc(places_ready, 1)


            def wg_largest():
                dve.wait_ge(wg_summed, 1)
                nc.vector.tensor_reduce(wg_norm[:, 0:1], bank[ROUTER][:, 0:KC * E], AX_X, ALU.max
                                        ).then_inc(wg_max_taken, 1)
                dve.wait_ge(wg_max_taken, 1)
                nc.vector.tensor_scalar(wg_norm[:, 1:2], wg_norm[:, 0:1], 1.05, 2.0 ** -60, ALU.mult, ALU.max
                                        ).then_inc(wg_norm_ready, 1)

            def powers(one, root, low, inverse_of_low):
                one.link(nc.vector.tensor_scalar(low.bitcast(I32), root.bitcast(I32), 0x7F800000, None,
                                                 ALU.bitwise_and))
                one.link(nc.vector.tensor_scalar(inverse_of_low.bitcast(I32), low.bitcast(I32), 0x7F800000, None,
                                                 ALU.bitwise_xor))

            def cut_router():
                one = Steps(dve, wg_step)
                dve.wait_ge(wg_root_ready, 1)
                powers(one, wg_norm[:, 2:3], wg_low2[:, :], wg_inv2[:, :])
                nc.vector.tensor_scalar(logit_scale[:, :], wg_low2[:, :], 2.0 ** -13 / X_SCALE, None, ALU.mult)
                one.link(nc.vector.tensor_scalar(wg_scaled[:, :, :], wg_sb[:, :, :], wg_inv2[:, 0:1], 2.0 ** 12,
                                                 ALU.mult, ALU.mult))
                one.link(nc.vector.tensor_copy(wg16[:, 0, :, :], wg_scaled[:, :, :]))
                nc.vector.tensor_tensor(wg16[:, 1, :, :], wg_scaled[:, :, :], wg16[:, 0, :, :], ALU.subtract
                                        ).then_inc(wg_ready, 1)
                dve.wait_ge(wg_ready, 1)

            def scales():
                one = Steps(dve, scale_step)
                dve.wait_ge(root_ready, 1)
                powers(one, norm[:, 2:3], low2[:, :], inv2[:, :])
                nc.vector.tensor_scalar(w_scale[:, :], inv2[:, :], 2.0 ** 12, None, ALU.mult)
                nc.vector.tensor_scalar(silu_scale[:, :], low2[:, :], 2.0 ** -13 / X_SCALE, None, ALU.mult)
                nc.vector.tensor_scalar(up_scale[:, :], inv2[:, :], 2.0 ** -9 / X_SCALE, None, ALU.mult)
                one.link(nc.vector.tensor_tensor(cube2[:, :], low2[:, :], low2[:, :], ALU.mult))
                one.link(nc.vector.scalar_tensor_tensor(y_scale[:, :], cube2[:, :], 2.0 ** -19, low2[:, :],
                                                        ALU.mult, ALU.mult))
                dve.sem_inc(w_low, DVE_PIECES)

            def low_weights(n, pieces):
                for piece in pieces:
                    e, j = (n - FIRST_CUT) * PAIR + piece // 3, piece % 3
                    dve.wait_ge(w_high, e * 3 + (j + 1))
                    nc.vector.scalar_tensor_tensor(
                        halves[:, bass.ds(e * (2 * SLOT) + (2 * j + 1) * PIECE, PIECE)],
                        weights[:, bass.ds((e + 1) * SLOT + j * PIECE, PIECE)], w_scale[:, 0:1],
                        halves[:, bass.ds(e * (2 * SLOT) + 2 * j * PIECE, PIECE)], ALU.mult, ALU.subtract
                    ).then_inc(w_low, 1)

            table = Steps(dve, table_step)

            def shared_out(c0, c1, number):
                n = c1 - c0
                table.link(nc.vector.tensor_tensor(upto[:, :, :], up_to[:, :, :],
                                                   number[:, :].unsqueeze(1).to_broadcast([P, E, E]), ALU.mult))
                table.link(nc.vector.tensor_reduce(ends[:, :], upto[:, :, :], AX_X, ALU.add))
                table.link(nc.vector.tensor_tensor(
                    past[:, 0:n, :], tile_no[:, 0:n].unsqueeze(2).to_broadcast([P, n, E]),
                    ends[:, :].unsqueeze(1).to_broadcast([P, n, E]), ALU.is_ge))

            def located(c0, c1, taken, start):
                n = c1 - c0
                table.mark(nc.vector.tensor_reduce(tile_expert[:, c0:c1], past[:, 0:n, :], AX_X, ALU.add))
                table.link(nc.vector.tensor_tensor(past_coef[:, 0:n, :], past[:, 0:n, :],
                                                   taken[:, :].unsqueeze(1).to_broadcast([P, n, E]), ALU.mult))
                table.link(nc.vector.tensor_reduce(tile_tmp[:, 0, 0:n], past_coef[:, 0:n, :], AX_X, ALU.add))
                table.mark(nc.vector.tensor_tensor(tile_tmp[:, 1, 0:n], tile_no[:, 0:n], tile_tmp[:, 0, 0:n],
                                                   ALU.subtract))
                table.link(nc.vector.tensor_scalar(tile_tmp[:, 2, 0:n], tile_expert[:, c0:c1], float(E),
                                                   float(TILE), ALU.is_lt, ALU.mult))
                table.link(nc.vector.scalar_tensor_tensor(tile_tmp[:, 3, 0:n], tile_tmp[:, 1, 0:n], start,
                                                          tile_tmp[:, 2, 0:n], ALU.add, ALU.mult))
                nc.vector.scalar_tensor_tensor(tile_row[:, c0:c1], tile_expert[:, c0:c1], float(REGION),
                                               tile_tmp[:, 3, 0:n], ALU.mult, ALU.add)
                nc.vector.tensor_scalar(tile_weights[:, c0:c1], tile_expert[:, c0:c1], float(E - 1),
                                        float(2 * SLOT), ALU.min, ALU.mult).then_inc(tiles_ready, 1)

            def counted(times, dst, rounding):
                dve.wait_ge(counts_ready, times)
                table.link(nc.vector.tensor_copy(count[:, :], bank[ROUTER if times == 2 else SUM][:, 0:E]))
                if times == 2:
                    table.link(nc.vector.tensor_tensor(expert_tmp[:, 0, :], count[:, :], region_of[:, :], ALU.add))
                    nc.vector.tensor_copy(pad_at[:, :], expert_tmp[:, 0, :]).then_inc(pad_at_ready, 1)
                table.link(nc.vector.tensor_scalar(count_i[:, 0, :], count[:, :], float(rounding), None, ALU.add))
                table.link(nc.vector.tensor_scalar(count_i[:, 1, :], count_i[:, 0, :], TILE.bit_length() - 1, None,
                                                   ALU.logical_shift_right))
                table.link(nc.vector.tensor_copy(dst[:, :], count_i[:, 1, :]))

            def early_table():
                counted(1, full, 0)
                shared_out(0, EARLY, full)
                located(0, EARLY, full, 0.0)
                table.mark(nc.vector.memset(first[:, E:E + 1], 0.0))
                table.link(nc.vector.tensor_tensor(expert_tmp[:, 0, :], full[:, :], ends[:, :], ALU.subtract))
                table.link(nc.vector.tensor_scalar(expert_tmp[:, 1, :], expert_tmp[:, 0, :], float(EARLY), 0.0,
                                                   ALU.add, ALU.max))
                table.link(nc.vector.tensor_tensor(first[:, 0:E], expert_tmp[:, 1, :], full[:, :], ALU.min))

            def late_table():
                counted(2, whole, TILE - 1)
                table.mark(nc.vector.tensor_tensor(left[:, :], whole[:, :], first[:, 0:E], ALU.subtract))
                table.link(nc.vector.tensor_tensor(coef[:, :], whole[:, :], first[:, 1:E + 1], ALU.subtract))
                shared_out(EARLY, NT, left)

            def read_meta(i, par):
                dve.wait_ge(rows_loaded[par], (i - par) * 8 + 16)
                if not is_first(i, 2):
                    dve.wait_ge(y_added, (i - 1) * 32)
                nc.vector.tensor_copy(target[:, par, :], xr[:, par, :, TOKEN].bitcast(I32))
                nc.vector.tensor_scalar(own[:, par, :], xr[:, par, :, FIRST], tile_expert[:, bass.ds(i, 1)], 2.0,
                                        ALU.is_equal, ALU.mult).then_inc(own_ready, 1)
                dve.wait_ge(own_ready, i + 1)
                nc.vector.scalar_tensor_tensor(margin[:, par, :], own[:, par, :], 1.0, xr[:, par, :, MARGIN],
                                               ALU.subtract, ALU.mult).then_inc(margin_ready, 1)

            def tile(i, par, midway=lambda: None, before_y=lambda: None):
                def low(hc):
                    dve.wait_ge(hid_high, i * HC + hc + 1)
                    nc.vector.tensor_tensor(hh[:, par, 1, hc, :], hid[:, hc, :], hh[:, par, 0, hc, :],
                                            ALU.subtract).then_inc(hid_low, 1)

                for hc in range(HC):
                    if hc == 2:
                        midway()
                    if hc == HC - 1:
                        read_meta(i, par)
                    dve.wait_ge(silu_ready, i * HC + hc + 1)
                    if not is_first(i):
                        dve.wait_ge(hid_low, (i - 1) * HC + hc + 1)
                    nc.vector.scalar_tensor_tensor(hid[:, hc, :], bank[hc][:, TILE:2 * TILE], up_scale[:, 0:1],
                                                   silu[:, hc % 2, :], ALU.mult, ALU.mult).then_inc(hid_ready, 1)
                    if hc >= 1:
                        low(hc - 1)
                low(HC - 1)
                before_y()
                if not is_first(i):
                    scale_y(i - 1, 1 - par)
                dve.wait_ge(tanh_ready, i + 1)
                nc.vector.tensor_scalar(gate[:, par, :], tanh[:, par, :], 1.0, y_scale[:, 0:1], ALU.add, ALU.mult
                                        ).then_inc(gate_ready, 1)

            def scale_y(i, par):
                dve.wait_ge(gate_ready, i + 1)
                dve.wait_ge(down_ready, i + 1)
                for c in range(2):
                    last = nc.vector.tensor_scalar(y[:, par, c, :], bank[DOWN[par]][:, c * D:(c + 1) * D],
                                                   gate[:, par, c:c + 1], None, ALU.mult)
                last.then_inc(y_ready, 1)

            dve.wait_ge(consts_ready, 1)
            statistics1(0, 0)
            inverse(0, 0, std1_ready, norm1_ready, 1.0)

            def lead_step(n, par, kind):
                def low(*pieces):
                    if kind in ("scales", "cut"):
                        low_weights(n, pieces)

                def square(k):
                    if kind not in ("squares", "scales") or n == 0:
                        return
                    dve.wait_ge(w_loaded[n - 1], 48 * PAIR)
                    if n >= 2:
                        dve.wait_ge(squares_summed, n - 1)
                    end = ((n - 1) * PAIR + k + 2) * SLOT
                    piece = weights[:, end - PIECE:end]
                    nc.vector.tensor_tensor(squares[:, k, SLOT - PIECE:SLOT], piece, piece, ALU.mult
                                            ).then_inc(squares_dve, 1)

                statistics1(n + 1, 1 - par)
                if not is_first(n, 2):
                    route(n - 2, par)
                inverse(n + 1, 0, std1_ready, norm1_ready, 1.0)
                if is_first(n):
                    wg_largest()
                residual(n, par, range(0, 2))
                if not is_first(n, 2):
                    places(n - 2, par)
                if kind == "cut":
                    low(0)
                square(0)
                if kind == "scales":
                    square(1)
                residual(n, par, range(2, G))
                inverse(n, 1, std2_ready, norm2_ready, X_SCALE)
                if kind == "scales":
                    dve.wait_ge(squares_summed, SQUARES)
                    nc.vector.tensor_reduce(norm[:, 0:1], bank[SUM][:, :], AX_X, ALU.max).then_inc(sum_taken, 1)
                    dve.wait_ge(sum_taken, 1)
                    nc.vector.tensor_scalar(norm[:, 1:2], norm[:, 0:1], 1.05, 2.0 ** -60, ALU.mult, ALU.max
                                            ).then_inc(norm_ready, 1)
                else:
                    square(1)
                if is_first(n):
                    cut_router()
                else:
                    take_rows(n - 1)
                if kind == "scales":
                    scales()
                    low(0)
                low(1, 2, 3, 4)

            def step(n, par, kind):
                if kind == "last":
                    inverse(n - 1, 1, std2_ready, norm2_ready, X_SCALE)
                    residual(n, par)
                    take_rows(n - 1)
                    inverse(n, 1, std2_ready, norm2_ready, X_SCALE)
                    route(n - 1, 1 - par)
                    places(n - 1, 1 - par)
                elif kind == "end":
                    take_rows(n - 1)
                    route(n - 1, 1 - par)
                elif kind == "tiles":
                    residual(n, par, range(0, 2))
                    if not is_first(n, LEAD + 2):
                        inverse(n - 1, 1, std2_ready, norm2_ready, X_SCALE)
                    statistics1(n + 1, 1 - par)
                    if is_first(n, LEAD + 2):
                        places(n - 2, par)
                    residual(n, par, range(2, G))
                    inverse(n + 1, 0, std1_ready, norm1_ready, 1.0)
                    tile(*early(n, par, 0), before_y=lambda: take_rows(n - 1))
                    route(n - 1, 1 - par)
                    tile(*early(n, par, 1), midway=lambda: places(n - 1, 1 - par))
                else:
                    lead_step(n, par, kind)

            def table_and_route():
                early_table()
                route(LEAD - 1, (LEAD - 1) % 2)

            def last_places():
                places(NG - 1, (NG - 1) % 2)

            phase1_steps(dve, step, table_and_route, steps)
            tiles_after(dve, lambda i, par: tile(i, par, midway=last_places if is_first(i, INTERLEAVED + 1) else lambda: None),
                        {INTERLEAVED: late_table, INTERLEAVED + 1: lambda: located(EARLY, NT, coef, first[:, 0:1])})
            scale_y(NT - 1, (NT - 1) % 2)

        @block.tensor
        def _(pe):
            pe.wait_ge(consts_ready, 1)
            pe.wait_ge(adj_half, 1)
            nc.tensor.transpose(bank[TURN][:, 0:P], adj_sb[:, :], ident32[:, :]).then_inc(adj_turned, 1)
            pe.wait_ge(wg_squared, 1)
            nc.tensor.matmul(bank[ROUTER][:, 0:KC * E], ones[:, :], wg_squares[:, :, :].rearrange("p c e -> p (c e)"),
                             start=True, stop=True).then_inc(wg_summed, 1)
            pe.wait_ge(setup_ready, 1)

            def z(n, par, t):
                pe.wait_ge(xn_ready, n * G + t + 1)
                for c in range(KC):
                    mm = nc.tensor.matmul(bank[t % 2][:, c * P:(c + 1) * P], xn[:, par, t, c * P:(c + 1) * P],
                                          adj_t[:, :], start=True, stop=True)
                mm.then_inc(z_ready, 1)

            def gnn(n, t):
                pe.wait_ge(zt_ready, n * G + t + 1)
                if not (is_first(n) and t < 2):
                    pe.wait_ge(h1_done, n * G + t - 1)
                if is_first(n) and t == 0:
                    pe.wait_ge(gnn_loaded, 16)
                    pe.wait_ge(bias_moved, 48)
                o = bank[2 + t % 2][:, 0:D]
                nc.tensor.matmul(o, ones[0:3, :], bias3[:, :], start=True, stop=False)
                for c in range(KC):
                    mm = nc.tensor.matmul(o, zt[:, t % 2, c * P:(c + 1) * P], gw_sb[:, c, :],
                                          start=False, stop=(c == KC - 1))
                mm.then_inc(gnn_ready, 1)

            def turn_rows(n, par, half):
                pe.wait_ge(low_ready, n * G + 2 * half + 2)
                o = bank[half][:, :].bitcast(F16)
                for t in range(2):
                    for part in range(2):
                        for c in range(KC):
                            at = ((t * 2 + part) * KC + c) * P
                            mm = nc.tensor.transpose(o[:, at:at + P], rows16[:, par, 2 * half + t,
                                                                             part * D + c * P:part * D + (c + 1) * P],
                                                     ident16[:, :])
                mm.then_inc(rows_turned, 1)

            def router(n, half):
                pe.wait_ge(rows_taken[half], n + 1)
                if half == 0:
                    if is_first(n):
                        pe.wait_ge(wg_ready, 1)
                    else:
                        pe.wait_ge(places_ready, n)
                for t in range(2):
                    at = (2 * half + t) * E
                    terms = [(c, a, b) for c in range(KC) for a, b in ((0, 0), (0, 1), (1, 0))]
                    for j, (c, a, b) in enumerate(terms):
                        mm = nc.tensor.matmul(bank[ROUTER][:, at:at + E], rows_t[:, half, t, a, c, :], wg16[:, b, c, :],
                                              start=(j == 0), stop=(j == len(terms) - 1))
                mm.then_inc(logits_ready, 1)

            def picks_before(n, par):
                pe.wait_ge(picks_ready, n + 1)
                o = bank[ROUTER]
                nc.tensor.matmul(o[:, 0:G * E], before[:, :], picks[:, :, :].rearrange("p t e -> p (t e)"),
                                 start=True, stop=False)
                for t in range(G - 1):
                    nc.tensor.matmul(o[:, (t + 1) * E:G * E], ones[:, :],
                                     picks[:, t, :].unsqueeze(1).to_broadcast([P, G - 1 - t, E]),
                                     start=False, stop=False)
                nc.tensor.matmul(o[:, 0:G * E], ones[:, :], running[:, par, :].unsqueeze(1).to_broadcast([P, G, E]),
                                 start=False, stop=True).then_inc(before_ready, 1)

            def sum_squares(n):
                for k in range(PAIR):
                    pe.wait_ge(squares_act, (n * PAIR + k + 1) * 2)
                    pe.wait_ge(squares_dve, n * PAIR + k + 1)
                    for j in range(SLOT // 512):
                        mm = nc.tensor.matmul(bank[SUM][:, :], ones[:, :], squares[:, k, j * 512:(j + 1) * 512],
                                              start=(n == 0 and k == 0 and j == 0),
                                              stop=(n == SQUARES - 1 and k == PAIR - 1 and j == SLOT // 512 - 1))
                mm.then_inc(squares_summed, 1)

            def counts(groups, in_bank):
                pe.wait_ge(running_ready, groups)
                pe.wait_ge(places_ready, groups)
                nc.tensor.matmul(bank[in_bank][:, 0:E], ones[:, :], running[:, groups % 2, :], start=True, stop=True
                                 ).then_inc(counts_ready, 1)

            def turn_x(i, par):
                pe.wait_ge(rows_loaded[par], (i - par) * 8 + 16)
                if not is_first(i):
                    pe.wait_ge(xt_ready, i)
                o = bank[TURN][:, :].bitcast(F16)
                for c in range(2):
                    for part in range(2):
                        for k in range(KC):
                            at = (part * KC + k) * TILE + c * P
                            mm = nc.tensor.transpose(o[:, at:at + P],
                                                     xr16[:, par, c, part * D + k * P:part * D + (k + 1) * P],
                                                     ident16[:, :])
                mm.then_inc(x_turned, 1)

            def weights_of(i):
                return pe.value_load(tile_weights[0:1, bass.ds(i, 1)], min_val=0, max_val=(E - 1) * 2 * SLOT)

            def down(i, par):
                w = weights_of(i)
                pe.wait_ge(hid_low, (i + 1) * HC)
                if not is_first(i, 2):
                    pe.wait_ge(y_ready, i - 1)
                for c in range(2):
                    terms = [(hc, a, b) for hc in range(HC) for a, b in ((0, 0), (0, 1), (1, 0))]
                    for j, (hc, a, b) in enumerate(terms):
                        mm = nc.tensor.matmul(bank[DOWN[par]][:, c * D:(c + 1) * D],
                                              hh[:, par, a, hc, c * P:(c + 1) * P],
                                              halves[:, bass.ds(w + ((4 + b) * PIECE + hc * D), D)],
                                              start=(j == 0), stop=(j == len(terms) - 1))
                mm.then_inc(down_ready, 1)

            def tile(i, par, w=None, turn_next=True, h1_taken=None, midway=lambda: None):
                if w is None:
                    w = weights_of(i)
                pe.wait_ge(xt_ready, i + 1)
                for hc in range(HC):
                    if not is_first(i):
                        pe.wait_ge(hid_ready, (i - 1) * HC + hc + 1)
                    if hc == 2:
                        midway()
                    if hc == 2 and h1_taken is not None:
                        pe.wait_ge(h1_done, h1_taken)
                    for side in range(2):
                        terms = [(k, a, b) for k in range(KC) for a, b in ((0, 0), (0, 1), (1, 0))]
                        for j, (k, a, b) in enumerate(terms):
                            mm = nc.tensor.matmul(
                                bank[hc][:, side * TILE:(side + 1) * TILE],
                                halves[:, bass.ds(w + ((2 * side + a) * PIECE + k * HID + hc * P), P)],
                                xt[:, par, b, k, :], start=(j == 0), stop=(j == len(terms) - 1))
                    mm.then_inc(up_ready, 1)
                if turn_next and not (isinstance(i, int) and i == NT - 1):
                    turn_x(i + 1, 1 - par)
                if not is_first(i):
                    down(i - 1, 1 - par)

            def finish(n, par, before_router=lambda: None):
                turn_rows(n, par, 0)
                turn_rows(n, par, 1)
                before_router()
                router(n, 0)
                router(n, 1)

            def banks_free(i):
                pe.wait_ge(hid_ready, (i + 1) * HC)

            def gnn_products(n, par, before_gnn=lambda t: None):
                z(n, par, 0)
                for t in range(G):
                    if t + 1 < G:
                        z(n, par, t + 1)
                    before_gnn(t)
                    gnn(n, t)

            def step(n, par, kind):
                if kind == "end":
                    finish(n - 1, 1 - par, lambda: turn_x(INTERLEAVED, INTERLEAVED % 2))
                elif kind == "last":
                    gnn_products(n, par, lambda t: banks_free(INTERLEAVED - 1) if t == 0 else None)
                    finish(n - 1, 1 - par)
                    picks_before(n - 1, 1 - par)
                elif kind == "tiles":
                    a, a_par = early(n, par, 0)
                    b, b_par = early(n, par, 1)
                    w = None if is_first(n, LEAD + 2) else weights_of(a)

                    def before_gnn(t):
                        if t == 0 and not is_first(n, LEAD + 2):
                            turn_x(a, a_par)
                            banks_free(a - 1)
                        if t == 2 and is_first(n, LEAD + 2):
                            picks_before(n - 2, par)

                    gnn_products(n, par, before_gnn)
                    if is_first(n, LEAD + 2):
                        turn_x(a, a_par)
                        pe.wait_ge(tiles_ready, 1)
                        pe.wait_ge(w_low, DVE_PIECES * (CUTS + 1))
                        pe.wait_ge(w_low_pool, CUTS)
                    tile(a, a_par, w, False, (n + 1) * G)
                    w = weights_of(b)
                    pe.wait_ge(hid_ready, a * HC + 2)
                    finish(n - 1, 1 - par, lambda: turn_x(b, b_par))
                    tile(b, b_par, w, False, midway=lambda: picks_before(n - 1, 1 - par))
                    pe.wait_ge(hid_ready, b * HC + 2)
                else:
                    def before_gnn(t):
                        if t == 0 and kind in ("squares", "scales") and n >= 2:
                            sum_squares(n - 2)
                        if t == 2 and not is_first(n, 2):
                            picks_before(n - 2, par)

                    gnn_products(n, par, before_gnn)
                    if kind == "scales":
                        sum_squares(n - 1)
                    if not is_first(n):
                        finish(n - 1, 1 - par)

            def last_picks():
                picks_before(NG - 1, (NG - 1) % 2)

            phase1_steps(pe, step, lambda: counts(ROUTED, SUM))
            tiles_after(pe, lambda i, par: tile(i, par, midway=last_picks if is_first(i, INTERLEAVED + 1) else lambda: None),
                        {INTERLEAVED: lambda: counts(NG, ROUTER), EARLY - 1: lambda: pe.wait_ge(tiles_ready, 2)})
            down(NT - 1, (NT - 1) % 2)


_INS = ["x", "adj", "L0_gnn_weight", "L0_gnn_bias", "L0_ffn_Wg", "L0_ffn_bg", "L0_ffn_W1", "L0_ffn_W3", "L0_ffn_W2"]
PAD_ROWS = 2 * P


def kernel(**inputs):
    import numpy as _np
    import concourse.bacc as _bacc
    from concourse import mybir as _mybir
    from concourse.bass_utils import run_bass_kernel_spmd as _run

    nc = _bacc.Bacc("TRN2", target_bir_lowering=False, num_devices=1)
    arrays, args = {}, []
    for name in _INS:
        a = _np.ascontiguousarray(inputs[name])
        arrays[f"in_{name}_dram"] = a
        args.append(nc.dram_tensor(f"in_{name}_dram", a.shape, _mybir.dt.from_np(a.dtype), kind="ExternalInput").ap())
    b, n, d = inputs["x"].shape
    out = nc.dram_tensor("out_0_dram", (b * n + PAD_ROWS, d), F32, kind="ExternalOutput").ap()
    build(nc, *args, out)
    r = _run(nc, [arrays], core_ids=[0])
    return r.results[0]["out_0_dram"][:b * n].reshape(b, n, d)
```
